# Optimizing a Trainium2 kernel written in Bass

```python
import numpy as np
import jax
import jax.numpy as jnp

def _softmax(x, axis=-1):
    return jax.nn.softmax(x, axis=axis)

def _gelu(x):
    return jax.nn.gelu(x, approximate=True)

def _silu(x):
    return jax.nn.silu(x)

def _sigmoid(x):
    return jax.nn.sigmoid(x)

def _layernorm(x, axis=-1, eps=1e-05):
    m = jnp.mean(x, axis=axis, keepdims=True)
    v = jnp.var(x, axis=axis, keepdims=True)
    return (x - m) / jnp.sqrt(v + eps)

def _scatter_add(tgt, idx, src, axis=0):
    return tgt.at[idx].add(src)

def _segment_sum(src, seg, n):
    return jax.ops.segment_sum(src, seg, n)
kernel_name = 'mk_flamingo_gated_d1_seqx_r4_a1161e'

def setup_inputs(seed: int=0):
    np.random.seed(seed)
    _w = jnp.asarray

    def _rec_inputs():
        import jax
        import jax.numpy as jnp
        _rk = jax.random.key(seed)
        x = -0.0003929 + 0.9999 * jax.random.normal(jax.random.fold_in(_rk, 1), (4, 512, 1024), jnp.float32)
        _lenS = 512 - jax.random.randint(jax.random.fold_in(_rk, 7), (4,), 0, max(1, 512 // 4) + 1, jnp.int32)
        _lenS2 = 64 - jax.random.randint(jax.random.fold_in(_rk, 8), (4,), 0, max(1, 64 // 4) + 1, jnp.int32)
        _ctx_4096P = jax.random.normal(jax.random.fold_in(_rk, 11), (4, 16, 1024), jnp.float32)
        _ctx_4096c = jax.random.dirichlet(jax.random.fold_in(_rk, 511), 0.3 * jnp.ones((16,), jnp.float32), (4, 64))
        _ctx_4096t = jnp.einsum('bsk,bkd->bsd', _ctx_4096c, _ctx_4096P)
        _ctx_4096t = _ctx_4096t * jax.lax.rsqrt(jnp.mean(jnp.square(_ctx_4096t)) + 1e-12) * 0.953939
        ctx_4096 = 2.81802e-05 + 1.00001 * (_ctx_4096t + 0.3 * jax.random.normal(jax.random.fold_in(_rk, 611), (4, 64, 1024), jnp.float32))
        _g = jax.random.normal(jax.random.fold_in(_rk, 9001), (2, 1), jnp.float32)
        _g = jnp.sign(_g) * jnp.maximum(jnp.abs(_g), 1.0) + (_g == 0) * 1.0
        g_xattn = _g[0]
        g_ffn = _g[1]
        return (x, ctx_4096, g_xattn, g_ffn)
    x, ctx_4096, g_xattn, g_ffn = _rec_inputs()

    def _L0_xattn_setup():
        import jax, jax.numpy as jnp
        import numpy as np
        HID = 1024
        NHEAD = 32
        NKV = 8
        HDIM = 128
        G = NHEAD // NKV
        key = jax.random.key(seed)
        ks = jax.random.split(key, 6)
        s = 0.02
        B, L = (2, 512)
        return {'query': jax.random.normal(ks[0], (B, L, HID), jnp.float32), 'kv': jax.random.normal(ks[1], (B, L, HID), jnp.float32), 'Wq': jax.random.normal(ks[2], (HID, NHEAD * HDIM), jnp.float32) * s, 'bq': jnp.zeros((NHEAD * HDIM,), jnp.float32), 'Wkv': jax.random.normal(ks[3], (HID, 2 * NKV * HDIM), jnp.float32) * s, 'bkv': jnp.zeros((2 * NKV * HDIM,), jnp.float32), 'Wo': jax.random.normal(ks[4], (NHEAD * HDIM, HID), jnp.float32) * s, 'bo': jnp.zeros((HID,), jnp.float32)}
    _L0_xattn_all = _L0_xattn_setup()
    _L0_xattn_in = {k: v for k, v in _L0_xattn_all.items() if k in ('Wq', 'bq', 'Wkv', 'bkv', 'Wo', 'bo')}
    del _L0_xattn_all

    def _L0_ffn_setup():
        import jax, jax.numpy as jnp
        import numpy as np
        M = 1024
        K = 1024

        def _make_2to4_mask(key, shape):
            scores = jax.random.normal(key, shape)
            g = scores.reshape(shape[0], shape[1] // 4, 4)
            rank = jnp.argsort(jnp.argsort(-jnp.abs(g), axis=-1), axis=-1)
            return (rank < 2).reshape(shape).astype(jnp.float32)
        key = jax.random.key(seed)
        k_x, k_w12, k_b12, k_w3, k_b3, k_m = jax.random.split(key, 6)
        x = jax.random.normal(k_x, (4, 512, K), dtype=jnp.float32)
        w12_dense = jax.random.normal(k_w12, (2 * M, K), dtype=jnp.float32) * (1.0 / np.sqrt(K))
        mask12 = _make_2to4_mask(k_m, (2 * M, K))
        w12 = w12_dense * mask12
        b12 = jax.random.normal(k_b12, (2 * M,), dtype=jnp.float32) * 0.01
        w3 = jax.random.normal(k_w3, (M, M), dtype=jnp.float32) * (1.0 / np.sqrt(M))
        b3 = jax.random.normal(k_b3, (M,), dtype=jnp.float32) * 0.01
        return {'x': x, 'w12': w12, 'b12': b12, 'w3': w3, 'b3': b3}
    _L0_ffn_all = _L0_ffn_setup()
    _L0_ffn_in = {k: v for k, v in _L0_ffn_all.items() if k in ('w12', 'b12', 'w3', 'b3')}
    del _L0_ffn_all
    return {'x': x, 'ctx_4096': ctx_4096, 'g_xattn': g_xattn, 'g_ffn': g_ffn, 'L0_xattn_Wq': _L0_xattn_in['Wq'], 'L0_xattn_bq': _L0_xattn_in['bq'], 'L0_xattn_Wkv': _L0_xattn_in['Wkv'], 'L0_xattn_bkv': _L0_xattn_in['bkv'], 'L0_xattn_Wo': _L0_xattn_in['Wo'], 'L0_xattn_bo': _L0_xattn_in['bo'], 'L0_ffn_w12': _L0_ffn_in['w12'], 'L0_ffn_b12': _L0_ffn_in['b12'], 'L0_ffn_w3': _L0_ffn_in['w3'], 'L0_ffn_b3': _L0_ffn_in['b3']}

def reference(x, ctx_4096, g_xattn, g_ffn, L0_xattn_Wq, L0_xattn_bq, L0_xattn_Wkv, L0_xattn_bkv, L0_xattn_Wo, L0_xattn_bo, L0_ffn_w12, L0_ffn_b12, L0_ffn_w3, L0_ffn_b3):
    import jax
    import jax.numpy as jnp

    def _L0_xattn_ref(query, kv, Wq, bq, Wkv, bkv, Wo, bo):
        import jax, jax.numpy as jnp
        import numpy as np
        HID = 1024
        NHEAD = 32
        NKV = 8
        HDIM = 128
        G = NHEAD // NKV
        B, L, _ = query.shape
        Lk = kv.shape[1]
        scale = jnp.asarray(1.0 / np.sqrt(HDIM), query.dtype)
        q = (query @ Wq + bq).reshape(B, L, NKV, G, HDIM)
        k_, v_ = jnp.split(kv @ Wkv + bkv, 2, axis=-1)
        k = k_.reshape(B, Lk, NKV, HDIM)
        v = v_.reshape(B, Lk, NKV, HDIM)
        scores = jnp.einsum('blkgd,bmkd->bkglm', q, k) * scale
        attn = jax.nn.softmax(scores, axis=-1)
        o = jnp.einsum('bkglm,bmkd->blkgd', attn, v).reshape(B, L, NHEAD * HDIM)
        return o @ Wo + bo

    def _L0_ffn_ref(x, w12, b12, w3, b3):
        import jax, jax.numpy as jnp
        import numpy as np
        M = 1024
        K = 1024

        def _make_2to4_mask(key, shape):
            scores = jax.random.normal(key, shape)
            g = scores.reshape(shape[0], shape[1] // 4, 4)
            rank = jnp.argsort(jnp.argsort(-jnp.abs(g), axis=-1), axis=-1)
            return (rank < 2).reshape(shape).astype(jnp.float32)
        x12 = jnp.einsum('bsk,mk->bsm', x, w12) + b12
        x1, x2 = jnp.split(x12, 2, axis=-1)
        x4 = jax.nn.silu(x1) * x2
        return jnp.einsum('bsm,nm->bsn', x4, w3) + b3
    x = x + jnp.tanh(g_xattn[0]) * _L0_xattn_ref(_layernorm(x, axis=-1), ctx_4096, L0_xattn_Wq, L0_xattn_bq, L0_xattn_Wkv, L0_xattn_bkv, L0_xattn_Wo, L0_xattn_bo)
    x = x + jnp.tanh(g_ffn[0]) * _L0_ffn_ref(_layernorm(x, axis=-1), L0_ffn_w12, L0_ffn_b12, L0_ffn_w3, L0_ffn_b3)
    return x

_drawn_inputs = setup_inputs


def setup_inputs(seed=0):
    import zlib

    import numpy as np

    out = dict(_drawn_inputs(seed))
    spreads = {'L0_xattn_bq': (0.0, 0.8), 'L0_xattn_bkv': (0.0, 0.1), 'L0_xattn_bo': (0.0, 0.1)}
    factors = {'L0_ffn_b12': 8.0, 'L0_ffn_b3': 6.83}
    for name, (base, spread) in spreads.items():
        noise = np.random.default_rng([zlib.crc32(name.encode()), seed]).standard_normal(out[name].shape)
        drawn = base * np.exp(spread * noise) if base else spread * noise
        out[name] = jnp.asarray(drawn.astype(out[name].dtype))
    for name, factor in factors.items():
        out[name] = (out[name] * factor).astype(out[name].dtype)
    return out
```

```python
from contextlib import ExitStack

import numpy as np

import concourse.bass as bass
from concourse import mybir

F32 = mybir.dt.float32
F32R = mybir.dt.float32r
ALU = mybir.AluOpType
ACT = mybir.ActivationFunctionType
AX = mybir.AxisListType

P = 128
BATCH, SEQ, HID = 4, 512, 1024
KEYS = 64
HEADS, GROUPS, HDIM = 32, 8, 128
GH = HEADS // GROUPS
PASSES = 2
PB = BATCH // PASSES
PTOK = PB * SEQ
TILES = PTOK // P
BT = SEQ // P
MC = HID // P
FF = 1024
FC = FF // P
HK = GH * KEYS
KC = HK // P
PK = PB * KEYS
HALF = 512
KVJ = 2 * GROUPS
EPS = 1e-5
SCALE = 1.0 / float(np.sqrt(HDIM))

W_KV = KVJ
W_LN = 2 * TILES
W_C, W_M, W_V = 2, GH * 2, PB * KC * 2
W_G = W_C + W_M + W_V
G_BANKS = [4, 5] + [0, 1, 2, 3] * (W_M // 4) + [0, 1, 4, 5] * (W_V // 4)
LN_BANKS = [0, 1, 2, 3] * (W_LN // 4)
W_PASS = 2 * W_LN + GROUPS * W_G
W_HI_PASS = 2 * W_LN + GROUPS * (W_M + W_V)
LN_STEPS = 7
CREDIT = 2


def build(nc, x, ctx_t, g_xattn, g_ffn, wq_t, bq, wkv, bkv, wo, bo, w12, b12, w3, b3, ident_in, out):
    with ExitStack() as stack:
        sem = lambda name: stack.enter_context(nc.semaphore(name))
        bank = lambda name: stack.enter_context(nc.psum_tensor(name, [P, HALF], F32))

        KB = 1024
        arena = stack.enter_context(nc.sbuf_tensor("arena", [P, 206 * KB // 4], F32))
        base = nc.sbuf_base - 206 * KB
        top = [0]

        def at(name, shape, dt, offset=None):
            size = 4 * int(np.prod(shape[1:]))
            start = top[0] if offset is None else offset
            if offset is None:
                top[0] += -(-size // 32) * 32
            assert start + size <= 206 * KB, name
            return nc.alloc_sbuf_tensor_at(name, shape, dt, offset=base + start)

        xt_hi = at("xt_hi", [P, MC, PTOK], F32R)
        xt_lo = at("xt_lo", [P, MC, PTOK], F32R)
        work_hi = at("work_hi", [P, MC * PTOK], F32R)
        work_lo = at("work_lo", [P, MC * PTOK], F32R)
        attn_at = top[0]
        acc = at("acc", [P, TILES, HID], F32)
        wq_sb = at("wq_sb", [P, GH, HID], F32)
        wo_at = top[0]
        wo_sb = at("wo_sb", [P, GH, HID], F32)
        tmp_at = top[0]
        kvg = at("kvg", [P, 2, PK], F32)
        sbias = at("sbias", [P, PB, GH, KEYS], F32)
        probs = at("probs", [P, 4, HK], F32)
        pt_hi = at("pt_hi", [P, 2, KC, P], F32R)
        pt_lo = at("pt_lo", [P, 2, KC, P], F32R)
        ident = at("ident", [P, P], F32)
        bqg = at("bqg", [P, GH], F32)
        bkv_sb = at("bkv_sb", [P, KVJ], F32)
        b12_sb = at("b12_sb", [P, 2 * FC], F32)
        gates = at("gates", [P, 2], F32)
        tanh_g = at("tanh_g", [P, 2], F32)
        stats = at("stats", [P, TILES, 2, 6], F32)
        mean_var = at("mean_var", [P, TILES, 2], F32)
        var_eps = at("var_eps", [P, TILES], F32)
        rstd = at("rstd", [P, TILES], F32)
        newton = at("newton", [P, TILES], F32)
        row_max = at("row_max", [P, 2, GH], F32)
        row_sum = at("row_sum", [P, 2, GH], F32)
        ctx_sb = at("ctx_sb", [P, MC, BATCH * KEYS], F32, wo_at + 8 * KB)
        kv_out = at("kv_out", [P, 2, BATCH * KEYS], F32, tmp_at + 1 * KB)
        bias_row = at("bias_row", [P, HID], F32, tmp_at + 3 * KB)
        w3a_hi = at("w3a_hi", [P, FC, HALF], F32R, attn_at)
        w3a_lo = at("w3a_lo", [P, FC, HALF], F32R, attn_at + 16 * KB)
        w12_hi = at("w12_hi", [P, 2, MC, P], F32R, attn_at + 32 * KB)
        w12_lo = at("w12_lo", [P, 2, MC, P], F32R, attn_at + 40 * KB)
        resid = at("resid", [P, 4, HALF], F32, wo_at)
        w12_raw = at("w12_raw", [P, 2, HID], F32, wo_at + 8 * KB)
        silu_sb = at("silu_sb", [P, 2, HALF], F32, tmp_at)
        hid_sb = at("hid_sb", [P, 2, HALF], F32, tmp_at + 4 * KB)
        w3_raw = at("w3_raw", [P, HALF], F32, tmp_at + 8 * KB)

        m_hi = work_hi[:, 0:MC * PB * HK].rearrange("p (c b k) -> p c b k", c=MC, b=PB)
        m_lo = work_lo[:, 0:MC * PB * HK].rearrange("p (c b k) -> p c b k", c=MC, b=PB)
        v_hi = work_hi[:, MC * PB * HK:].rearrange("p (b c n) -> p b c n", b=PB, c=KC)
        v_lo = work_lo[:, MC * PB * HK:].rearrange("p (b c n) -> p b c n", b=PB, c=KC)
        h_hi = work_hi[:, :].rearrange("p (c t) -> p c t", c=FC)
        h_lo = work_lo[:, :].rearrange("p (c t) -> p c t", c=FC)
        w3b_hi = xt_hi[:, 0:FC // 2, :].rearrange("p c (u n) -> p (c u) n", u=2)
        w3b_lo = xt_lo[:, 0:FC // 2, :].rearrange("p c (u n) -> p (c u) n", u=2)
        x_norm = wo_sb

        ps_w = [bank("ps_w0"), bank("ps_w1")]
        ps_s = [bank("ps_s0"), bank("ps_s1")]
        ps_t = [bank("ps_t0"), bank("ps_t1")]
        wide = ps_w + ps_s + ps_t
        ps_o = [bank("ps_o0"), bank("ps_o1")]

        kv_dram = nc.dram_tensor("kv_scratch", (2, GROUPS, PASSES, P, PK), F32, kind="Internal").ap()
        x1_dram = nc.dram_tensor("x1_scratch", (BATCH * SEQ, HID), F32, kind="Internal").ap()

        kv_store = kv_dram.rearrange("k g q p m -> (k g) p q m")
        kv_load = kv_dram.rearrange("k g q p m -> (g q) p k m")
        x_tiles = x.rearrange("(q t p) n -> q t p n", q=PASSES, p=P)
        x1_tiles = x1_dram.rearrange("(q t p) n -> q t p n", q=PASSES, p=P)
        out_tiles = out.rearrange("(q t p) n -> q t p n", q=PASSES, p=P)
        wq_v = wq_t.rearrange("(g h p) n -> g p h n", g=GROUPS, p=P)
        wo_v = wo.rearrange("(g h p) n -> g p h n", g=GROUPS, p=P)
        w3_v = w3.rearrange("(f p) n -> f p n", p=P)

        consts_in = sem("consts_in")
        passed = sem("passed")
        gates_in = sem("gates_in")
        ctx_in = sem("ctx_in")
        wkv_in = [sem(f"wkv_in{s}") for s in range(4)]
        kv_stored = [sem(f"kv_stored{s}") for s in range(2)]
        x_in = [sem(f"x_in{t}") for t in range(TILES)]
        brow_in = sem("brow_in")
        brow_ready = sem("brow_ready")
        bias_added = sem("bias_added")
        x1_stored = sem("x1_stored")
        wq_in = sem("wq_in")
        wo_in = sem("wo_in")
        kvg_in = sem("kvg_in")
        tanh_ready = sem("tanh_ready")
        ln_step = sem("ln_step")
        std_ready = sem("std_ready")
        norm_ready = sem("norm_ready")
        w_ready = sem("w_ready")
        w_hi = sem("w_hi")
        w_free = sem("w_free")
        s_ready = sem("s_ready")
        s_free = sem("s_free")
        maxed = sem("maxed")
        shifted = sem("shifted")
        exped = sem("exped")
        summed = sem("summed")
        inverted = sem("inverted")
        probs_ready = sem("probs_ready")
        t_ready = sem("t_ready")
        pt_hi_ready = sem("pt_hi_ready")
        t_free = sem("t_free")
        o_ready = sem("o_ready")
        o_free = sem("o_free")
        w12_in = [sem("w12_in0"), sem("w12_in1")]
        w12_hi_ready = [sem("w12_hi_ready0"), sem("w12_hi_ready1")]
        w12_ready = [sem("w12_ready0"), sem("w12_ready1")]
        w3_in = sem("w3_in")
        w3_hi_ready = sem("w3_hi_ready")
        w3_ready = sem("w3_ready")
        w3b_in = [sem("w3b_in0"), sem("w3b_in1")]
        w3b_hi_ready = [sem("w3b_hi_ready0"), sem("w3b_hi_ready1")]
        w3b_ready = [sem("w3b_ready0"), sem("w3b_ready1")]
        gate_ready = sem("gate_ready")
        lin_ready = sem("lin_ready")
        silu_ready = sem("silu_ready")
        hid_ready = sem("hid_ready")
        hid_hi = sem("hid_hi")
        hid_lo = sem("hid_lo")
        resid_in = [sem(f"resid_in{s}") for s in range(4)]
        pass_over = sem("pass_over")
        out_stored = [sem(f"out_stored{s}") for s in range(4)]

        F2N = 2 * TILES
        T_PASS = GROUPS * TILES + F2N

        def freed(banks, n):
            same = [k for k in range(n) if banks[k] == banks[n]]
            return same[-1] + 1 if same else None

        def w_at(q, g, n):
            return q * W_PASS + g * W_G + (W_KV + W_LN + n)

        def alone(eng):
            eng.sem_inc(passed, 1)

        block = stack.enter_context(nc.Block())

        @block.sync
        def _(sp):
            sp.dma_start(ctx_sb[:, :, :], ctx_t.rearrange("p (c n) -> p c n", c=MC)).then_inc(ctx_in, 16)
            sp.dma_start(bkv_sb[:, :], bkv).then_inc(consts_in, 16)
            sp.dma_start(ident[:, :], ident_in).then_inc(consts_in, 16)
            sp.dma_start(b12_sb[:, :], b12).then_inc(consts_in, 16)
            sp.dma_start(gates[:, 0:1], g_xattn).then_inc(gates_in, 16)
            sp.dma_start(gates[:, 1:2], g_ffn).then_inc(gates_in, 16)
            for s in range(4):
                sp.dma_start(wq_sb[:, s, :], wkv[s]).then_inc(wkv_in[s], 16)
            with sp.Fori(1, KVJ // 4) as i:
                for s in range(4):
                    sp.wait_ge(w_ready, (i - 1) * 4 + (s + 1))
                    alone(sp)
                    sp.dma_start(wq_sb[:, s, :], wkv[i * 4 + s]).then_inc(wkv_in[s], 16)
            with sp.Fori(0, PASSES) as q:
                sp.wait_ge(pass_over, q + 1)
                for s in range(2):
                    sp.wait_ge(kv_stored[s], 16 * KVJ // 2)
                sp.dma_start(bias_row[:, :], bo).then_inc(brow_in, 16)
                with sp.Fori(0, GROUPS) as g:
                    sp.wait_ge(w_ready, w_at(q, g, W_C + W_M - W_G))
                    sp.dma_start(wq_sb[:, :, :], wq_v[g]).then_inc(wq_in, 16)
                    sp.wait_ge(w_ready, w_at(q, g, 0))
                    sp.dma_start(kvg[:, :, :], kv_load[g * PASSES + q]).then_inc(kvg_in, 16)
                    sp.dma_start(bqg[:, :], bq[g]).then_inc(kvg_in, 16)
                    sp.dma_start(wo_sb[:, :, :], wo_v[g]).then_inc(wo_in, 16)
                sp.wait_ge(t_ready, q * T_PASS + GROUPS * TILES)
                sp.dma_start(bias_row[:, :], b3).then_inc(brow_in, 16)
                with sp.Fori(0, FC) as f:
                    for u in range(2):
                        sp.wait_ge(w12_ready[u], q * FC + f + 1)
                        if u == 0:
                            sp.wait_ge(w_ready, q * W_PASS + (W_KV + W_LN + GROUPS * W_G))
                        alone(sp)
                        sp.dma_start(w12_raw[:, u, :], w12[f + u * FC]).then_inc(w12_in[u], 16)
                    sp.wait_ge(w3_ready, q * FC + f + 1)
                    sp.wait_ge(w_free, (q + 1) * W_PASS + (W_KV + CREDIT))
                    sp.dma_start(w3_raw[:, :], w3_v[f, :, 0:HALF]).then_inc(w3_in, 16)
                for s in range(2):
                    sp.wait_ge(w12_ready[s], (q + 1) * FC + 1)
                    alone(sp)
                sp.wait_ge(x1_stored, (q + 1) * (16 * TILES))
                for n in range(F2N):
                    half, t = divmod(n, TILES)
                    if n < FC:
                        if n >= 2:
                            sp.wait_ge(w3b_ready[n % 2], q * (FC // 2) + n // 2)
                        sp.dma_start(w12_raw[:, n % 2, 0:HALF], w3_v[n, :, HALF:]).then_inc(w3b_in[n % 2], 16)
                    if n >= 4:
                        sp.wait_ge(out_stored[n % 4], q * (16 * F2N // 4) + 16 * (n // 4))
                    sp.dma_start(resid[:, n % 4, :], x1_tiles[q, t, :, half * HALF:(half + 1) * HALF])\
                        .then_inc(resid_in[n % 4], 16)

        @block.gpsimd
        def _(pool):
            pool.sem_inc(pass_over, 1)
            for u in range(2):
                pool.sem_inc(w12_ready[u], 1)
            pool.sem_inc(w3_ready, 1)
            with pool.Fori(0, KVJ // 2) as i:
                for s in range(2):
                    pool.wait_ge(w_free, i * 2 + (s + 1 + CREDIT))
                    alone(pool)
                    pool.dma_start(kv_store[i * 2 + s],
                                   kv_out[:, s, :].rearrange("p (q m) -> p q m", q=PASSES))\
                        .then_inc(kv_stored[s], 16)
            pool.wait_ge(tanh_ready, 1)

            def add_bias(q, which):
                pool.wait_ge(brow_in, q * 32 + (16 * which + 16))
                alone(pool)
                nc.gpsimd.tensor_scalar(bias_row[:, :], bias_row[:, :], tanh_g[:, which:which + 1], None,
                                        ALU.mult).then_inc(brow_ready, 1)
                pool.wait_ge(brow_ready, q * 2 + (which + 1))
                for t in range(TILES):
                    pool.wait_ge(norm_ready, q * (2 * TILES) + (which * TILES + t + 1))
                    nc.gpsimd.tensor_tensor(acc[:, t, :], acc[:, t, :], bias_row[:, :], ALU.add)\
                        .then_inc(bias_added, 1)
                    if which == 1:
                        pool.wait_ge(bias_added, q * (2 * TILES) + (TILES + t + 1))
                        alone(pool)
                        pool.dma_start(x1_tiles[q, t], acc[:, t, :]).then_inc(x1_stored, 16)

            with pool.Fori(0, PASSES) as q:
                add_bias(q, 0)
                add_bias(q, 1)
                pool.wait_ge(x1_stored, (q + 1) * (16 * TILES))
                alone(pool)
                with pool.Fori(0, FC) as f:
                    for u in range(2):
                        pool.wait_ge(w12_hi_ready[u], q * FC + f + 1)
                        nc.gpsimd.tensor_tensor(w12_lo[:, u, :, :].rearrange("p c n -> p (c n)"),
                                                w12_raw[:, u, :],
                                                w12_hi[:, u, :, :].rearrange("p c n -> p (c n)").bitcast(F32),
                                                ALU.subtract).then_inc(w12_ready[u], 1)
                    pool.wait_ge(w3_hi_ready, q * FC + f + 1)
                    nc.gpsimd.tensor_tensor(w3a_lo[:, f, :], w3_raw[:, :], w3a_hi[:, f, :].bitcast(F32),
                                            ALU.subtract).then_inc(w3_ready, 1)
                for n in range(F2N):
                    if n < FC:
                        pool.wait_ge(w3b_hi_ready[n % 2], q * (FC // 2) + (n // 2 + 1))
                        nc.gpsimd.tensor_tensor(w3b_lo[:, n, :], w12_raw[:, n % 2, 0:HALF],
                                                w3b_hi[:, n, :].bitcast(F32), ALU.subtract)\
                            .then_inc(w3b_ready[n % 2], 1)
                    half, t = divmod(n, TILES)
                    pool.wait_ge(t_free, q * T_PASS + (GROUPS * TILES + n + 1 + CREDIT))
                    alone(pool)
                    pool.dma_start(out_tiles[q, t, :, half * HALF:(half + 1) * HALF], resid[:, n % 4, :])\
                        .then_inc(out_stored[n % 4], 16)
                for s in range(4):
                    pool.wait_ge(out_stored[s], (q + 1) * (16 * F2N // 4))
                    alone(pool)
                pool.sem_inc(pass_over, 1)

        @block.tensor
        def _(pe):
            def three_pass(ps, w_hi_ap, w_lo_ap, m_hi_ap, m_lo_ap, first, last):
                pe.matmul(ps, w_hi_ap, m_hi_ap, start=first, stop=False)
                pe.matmul(ps, w_hi_ap, m_lo_ap, start=False, stop=False)
                return pe.matmul(ps, w_lo_ap, m_hi_ap, start=False, stop=last)

            pe.wait_ge(ctx_in, 16)
            pe.wait_ge(consts_in, 48)
            with pe.Fori(0, KVJ // 4) as i:
                for s in range(4):
                    pe.wait_ge(wkv_in[s], i * 16 + 16)
                    pe.wait_ge(w_free, i * 4 + (s + 1))
                    for c in range(MC):
                        mm = pe.matmul(ps_w[s % 2][:, 0:BATCH * KEYS], wq_sb[:, s, c * P:(c + 1) * P],
                                       ctx_sb[:, c, :], start=(c == 0), stop=(c == MC - 1))
                    mm.then_inc(w_ready, 1)

            def transpose_tokens(q, which):
                for t in range(TILES):
                    pe.wait_ge(norm_ready, q * (2 * TILES) + (which * TILES + t + 1))
                    for half in range(2):
                        n = 2 * t + half
                        before = W_KV + which * (W_LN + GROUPS * W_G)
                        pe.wait_ge(w_free, q * W_PASS + (before + CREDIT + (freed(LN_BANKS, n) or 0)))
                        for k in range(4):
                            c = 4 * half + k
                            mm = pe.transpose(wide[LN_BANKS[n]][:, k * P:(k + 1) * P],
                                              x_norm[:, t % 2, c * P:(c + 1) * P], ident[:, :])
                        mm.then_inc(w_ready, 1)

            def scores(q, g, t):
                b = t // BT
                pe.wait_ge(s_free, q * (GROUPS * TILES) + g * TILES + (t + 1))
                for c in range(MC):
                    tok = slice(t * P, (t + 1) * P)
                    mm = three_pass(ps_s[t % 2][:, 0:HK], xt_hi[:, c, tok], xt_lo[:, c, tok],
                                    m_hi[:, c, b, :], m_lo[:, c, b, :], c == 0, c == MC - 1)
                mm.then_inc(s_ready, 1)

            def transpose_probs(q, g, t):
                pe.wait_ge(probs_ready, q * (GROUPS * TILES) + g * TILES + (t + 1))
                pe.wait_ge(t_free, q * T_PASS + g * TILES + (t + 1))
                for k in range(KC):
                    mm = pe.transpose(ps_t[t % 2][:, k * P:(k + 1) * P], probs[:, t % 4, k * P:(k + 1) * P],
                                      ident[:, :])
                mm.then_inc(t_ready, 1)

            def attend(q, g, t):
                b = t // BT
                pe.wait_ge(t_free, q * T_PASS + g * TILES + (t + 1 + CREDIT))
                for half in range(2):
                    cols = slice(half * HALF, (half + 1) * HALF)
                    pe.wait_ge(o_free, q * (GROUPS * TILES * 2) + g * (2 * TILES) + (2 * t + half + 1))
                    for k in range(KC):
                        mm = three_pass(ps_o[half][:, :], pt_hi[:, t % 2, k, :], pt_lo[:, t % 2, k, :],
                                        v_hi[:, b, k, cols], v_lo[:, b, k, cols], k == 0, k == KC - 1)
                    mm.then_inc(o_ready, 1)

            def wide_bank(q, g, n):
                before = freed(G_BANKS, n)
                if before is not None:
                    pe.wait_ge(w_free, w_at(q, g, CREDIT + before))
                elif G_BANKS[n] in (0, 1):
                    pe.wait_ge(w_free, w_at(q, g, CREDIT))
                elif G_BANKS[n] in (2, 3):
                    pe.wait_ge(s_free, q * (GROUPS * TILES) + g * TILES + CREDIT)
                else:
                    pe.wait_ge(t_free, q * T_PASS + g * TILES + CREDIT)
                return wide[G_BANKS[n]]

            with pe.Fori(0, PASSES) as q:
                transpose_tokens(q, 0)
                with pe.Fori(0, GROUPS) as g:
                    pe.wait_ge(kvg_in, q * (32 * GROUPS) + g * 32 + 32)
                    for n in range(W_C):
                        ps = wide_bank(q, g, n)
                        for k in range(2):
                            h = 2 * n + k
                            mm = pe.matmul(ps[:, k * PK:(k + 1) * PK],
                                           bqg[:, h:h + 1].to_broadcast([P, P]), kvg[:, 0, :],
                                           start=True, stop=True)
                        mm.then_inc(w_ready, 1)
                    pe.wait_ge(wq_in, q * (16 * GROUPS) + g * 16 + 16)
                    for n in range(W_M):
                        h, c4 = divmod(n, 2)
                        ps = wide_bank(q, g, W_C + n)
                        for k in range(4):
                            c = 4 * c4 + k
                            mm = pe.matmul(ps[:, k * PK:(k + 1) * PK],
                                           wq_sb[:, h, c * P:(c + 1) * P], kvg[:, 0, :],
                                           start=True, stop=True)
                        mm.then_inc(w_ready, 1)
                    pe.wait_ge(wo_in, q * (16 * GROUPS) + g * 16 + 16)
                    for n in range(W_V):
                        k, b, half = n // (2 * PB), n // 2 % PB, n % 2
                        ps = wide_bank(q, g, W_C + W_M + n)
                        for u in range(2):
                            mm = pe.matmul(ps[u * KEYS:(u + 1) * KEYS, :],
                                           kvg[:, 1, b * KEYS:(b + 1) * KEYS],
                                           wo_sb[:, 2 * k + u, half * HALF:(half + 1) * HALF],
                                           start=True, stop=True)
                        mm.then_inc(w_ready, 1)
                    pe.wait_ge(w_free, w_at(q, g, W_C + W_M + CREDIT))
                    for k in range(TILES + 3):
                        if k < TILES:
                            scores(q, g, k)
                        if k == 2:
                            pe.wait_ge(w_free, w_at(q, g, W_G + CREDIT))
                        if 0 <= k - 2 < TILES:
                            transpose_probs(q, g, k - 2)
                        if k >= 3:
                            attend(q, g, k - 3)
                transpose_tokens(q, 1)
                pe.wait_ge(w_free, (q + 1) * W_PASS + (W_KV + CREDIT))
                alone(pe)

                with pe.Fori(0, FC) as f:
                    for u in range(2):
                        pe.wait_ge(w12_ready[u], q * FC + f + 2)
                        for k in range(2):
                            if u == 0:
                                pe.wait_ge(silu_ready, q * (2 * FC) + f * 2 + (k + 1))
                            else:
                                pe.wait_ge(hid_ready, q * (2 * FC) + f * 2 + (k + 1))
                            ps = (ps_s, ps_o)[u][k]
                            tok = slice(k * HALF, (k + 1) * HALF)
                            for c in range(MC):
                                mm = three_pass(ps[:, :], w12_hi[:, u, c, :], w12_lo[:, u, c, :],
                                                xt_hi[:, c, tok], xt_lo[:, c, tok], c == 0, c == MC - 1)
                            mm.then_inc((gate_ready, lin_ready)[u], 1)
                pe.wait_ge(w3_ready, (q + 1) * FC + 1)
                pe.wait_ge(hid_lo, (q + 1) * (2 * FC) + CREDIT)
                for n in range(F2N):
                    half, t = divmod(n, TILES)
                    if half == 1 and t == 0:
                        for s in range(2):
                            pe.wait_ge(w3b_ready[s], (q + 1) * (FC // 2))
                    pe.wait_ge(t_free, q * T_PASS + (GROUPS * TILES + n + 1))
                    tok = slice(t * P, (t + 1) * P)
                    w3_hi_half, w3_lo_half = ((w3a_hi, w3a_lo), (w3b_hi, w3b_lo))[half]
                    for f in range(FC):
                        mm = three_pass(ps_t[n % 2][:, :], h_hi[:, f, tok], h_lo[:, f, tok],
                                        w3_hi_half[:, f, :], w3_lo_half[:, f, :], f == 0, f == FC - 1)
                    mm.then_inc(t_ready, 1)

        @block.scalar
        def _(act):
            act.sem_inc(silu_ready, CREDIT)
            act.wait_ge(gates_in, 32)
            nc.scalar.activation(tanh_g[:, :], gates[:, :], ACT.Tanh).then_inc(tanh_ready, 1)

            def split_tokens_hi(q, which):
                act.wait_ge(ln_step, q * (2 * LN_STEPS) + (which * LN_STEPS + 3))
                nc.scalar.activation(rstd[:, :], var_eps[:, :], ACT.Sqrt).then_inc(std_ready, 1)
                for n in range(W_LN):
                    t, half = divmod(n, 2)
                    before = W_KV + which * (W_LN + GROUPS * W_G)
                    act.wait_ge(w_ready, q * W_PASS + (before + n + 1))
                    nc.scalar.activation(xt_hi[:, 4 * half:4 * half + 4, t * P:(t + 1) * P],
                                         wide[LN_BANKS[n]][:, :].rearrange("p (c n) -> p c n", c=4), ACT.Copy)\
                        .then_inc(w_hi, 1)

            def split_w12_hi(q, f, u):
                act.wait_ge(w12_in[u], q * (16 * FC) + f * 16 + 16)
                nc.scalar.activation(w12_hi[:, u, :, :].rearrange("p c n -> p (c n)"), w12_raw[:, u, :],
                                     ACT.Copy).then_inc(w12_hi_ready[u], 1)

            def hidden_chunk(q, f, split_next):
                for k in range(2):
                    act.wait_ge(gate_ready, q * (2 * FC) + f * 2 + (k + 1))
                    alone(act)
                    nc.scalar.activation(silu_sb[:, k, :], ps_s[k][:, :], ACT.Silu,
                                         bias=b12_sb[:, bass.ds(f, 1)]).then_inc(silu_ready, 1)
                if split_next:
                    split_w12_hi(q, f + 1, 0)
                act.wait_ge(w3_in, q * (16 * FC) + f * 16 + 16)
                nc.scalar.activation(w3a_hi[:, bass.ds(f, 1), :].rearrange("p c n -> p (c n)"), w3_raw[:, :],
                                     ACT.Copy).then_inc(w3_hi_ready, 1)
                for k in range(2):
                    act.wait_ge(hid_ready, q * (2 * FC) + f * 2 + (k + 1 + CREDIT))
                    nc.scalar.activation(h_hi[:, bass.ds(f, 1), k * HALF:(k + 1) * HALF]
                                         .rearrange("p c n -> p (c n)"), hid_sb[:, k, :], ACT.Copy)\
                        .then_inc(hid_hi, 1)
                if split_next:
                    split_w12_hi(q, f + 1, 1)

            with act.Fori(0, PASSES) as q:
                act.wait_ge(pass_over, q + 1)
                alone(act)
                for t in range(TILES):
                    act.dma_start(acc[:, t, :], x_tiles[q, t]).then_inc(x_in[t], 16)
                split_tokens_hi(q, 0)
                with act.Fori(0, GROUPS) as g:
                    for n in range(W_M):
                        h, c4 = divmod(n, 2)
                        act.wait_ge(w_ready, w_at(q, g, W_C + n + 1))
                        nc.scalar.activation(m_hi[:, 4 * c4:4 * c4 + 4, :, h * KEYS:(h + 1) * KEYS],
                                             wide[G_BANKS[W_C + n]][:, :]
                                             .rearrange("p (c b k) -> p c b k", c=4, b=PB), ACT.Copy).then_inc(w_hi, 1)
                    for n in range(W_V):
                        k, b, half = n // (2 * PB), n // 2 % PB, n % 2
                        act.wait_ge(w_ready, w_at(q, g, W_C + W_M + n + 1))
                        nc.scalar.activation(v_hi[:, b, k, half * HALF:(half + 1) * HALF],
                                             wide[G_BANKS[W_C + W_M + n]][:, :], ACT.Copy).then_inc(w_hi, 1)
                    for k in range(TILES + 2):
                        if 0 <= k - 2 < TILES:
                            t = k - 2
                            act.wait_ge(t_ready, q * T_PASS + g * TILES + (t + 1))
                            nc.scalar.activation(pt_hi[:, t % 2, :, :].rearrange("p c n -> p (c n)"),
                                                 ps_t[t % 2][:, 0:HK], ACT.Copy).then_inc(pt_hi_ready, 1)
                        if k < TILES:
                            act.wait_ge(shifted, q * (GROUPS * TILES) + g * TILES + (k + 1))
                            nc.scalar.activation(probs[:, k % 4, :], probs[:, k % 4, :], ACT.Exp, scale=SCALE)\
                                .then_inc(exped, 1)
                split_tokens_hi(q, 1)
                act.wait_ge(x1_stored, (q + 1) * (16 * TILES))
                for u in range(2):
                    split_w12_hi(q, 0, u)
                with act.Fori(0, FC - 1) as f:
                    hidden_chunk(q, f, True)
                hidden_chunk(q, FC - 1, False)
                act.wait_ge(hid_lo, (q + 1) * (2 * FC) + CREDIT)
                for n in range(FC):
                    act.wait_ge(w3b_in[n % 2], q * (16 * FC // 2) + (16 * (n // 2) + 16))
                    nc.scalar.activation(w3b_hi[:, n, :], w12_raw[:, n % 2, 0:HALF], ACT.Copy)\
                        .then_inc(w3b_hi_ready[n % 2], 1)

        @block.vector
        def _(dve):
            for s in (w_free, s_free, t_free, o_free, hid_ready, hid_lo):
                dve.sem_inc(s, CREDIT)
            dve.wait_ge(consts_in, 48)
            def evacuate_kv(j, s):
                nc.vector.tensor_scalar(kv_out[:, s, :], ps_w[s][:, 0:BATCH * KEYS],
                                        bkv_sb[:, bass.ds(j, 1)], None, ALU.add).then_inc(w_free, 1)

            for s in range(2):
                dve.wait_ge(w_ready, s + 1)
                evacuate_kv(s, s)
            with dve.Fori(1, KVJ // 2) as i:
                for s in range(2):
                    dve.wait_ge(w_ready, i * 2 + (s + 1))
                    dve.wait_ge(kv_stored[s], i * 16)
                    evacuate_kv(i * 2 + s, s)

            def layer_norm(q, which):
                step = lambda k: q * (2 * LN_STEPS) + (which * LN_STEPS + k)
                for t in range(TILES):
                    if which == 0:
                        dve.wait_ge(x_in[t], q * 16 + 16)
                    for half in range(2):
                        last = nc.vector.bn_stats(stats[:, t, half, :], acc[:, t, half * HALF:(half + 1) * HALF])
                last.then_inc(ln_step, 1)
                dve.wait_ge(ln_step, step(1))
                alone(dve)
                for t in range(TILES):
                    last = nc.vector.bn_aggr(mean_var[:, t, :], stats[:, t, :, :].rearrange("p a b -> p (a b)"))
                last.then_inc(ln_step, 1)
                dve.wait_ge(ln_step, step(2))
                nc.vector.tensor_scalar(var_eps[:, :], mean_var[:, :, 1], EPS, None, ALU.add).then_inc(ln_step, 1)
                dve.wait_ge(std_ready, q * 2 + (which + 1))
                nc.vector.reciprocal(rstd[:, :], rstd[:, :]).then_inc(ln_step, 1)
                dve.wait_ge(ln_step, step(4))
                nc.vector.tensor_tensor(newton[:, :], rstd[:, :], rstd[:, :], ALU.mult).then_inc(ln_step, 1)
                dve.wait_ge(ln_step, step(5))
                nc.vector.scalar_tensor_tensor(out=newton[:, :], in0=newton[:, :], scalar=-0.5, in1=var_eps[:, :],
                                               op0=ALU.mult, op1=ALU.mult).then_inc(ln_step, 1)
                dve.wait_ge(ln_step, step(6))
                nc.vector.scalar_tensor_tensor(out=rstd[:, :], in0=newton[:, :], scalar=1.5, in1=rstd[:, :],
                                               op0=ALU.add, op1=ALU.mult).then_inc(ln_step, 1)
                dve.wait_ge(ln_step, step(7))
                before = W_KV + which * (W_LN + GROUPS * W_G)
                for t in range(TILES + 1):
                    if t < TILES:
                        if t >= 2:
                            dve.wait_ge(w_ready, q * W_PASS + (before + 2 * t - 2))
                        nc.vector.tensor_scalar(x_norm[:, t % 2, :], acc[:, t, :], mean_var[:, t, 0:1],
                                                rstd[:, t:t + 1], ALU.subtract, ALU.mult).then_inc(norm_ready, 1)
                    if t >= 1:
                        for half in range(2):
                            n = 2 * (t - 1) + half
                            dve.wait_ge(w_hi, q * W_HI_PASS + (which * (W_LN + GROUPS * (W_M + W_V)) + n + 1))
                            cols = (slice(None), slice(4 * half, 4 * half + 4), slice((t - 1) * P, t * P))
                            nc.vector.tensor_tensor(xt_lo[cols], wide[LN_BANKS[n]][:, :].rearrange("p (c n) -> p c n", c=4),
                                                    xt_hi[cols].bitcast(F32), ALU.subtract).then_inc(w_free, 1)

            def biased_scores(q, g, t):
                b = t // BT
                i = lambda k: q * (GROUPS * TILES) + g * TILES + (t + k)
                tile = probs[:, t % 4, :].rearrange("p (h m) -> p h m", h=GH)
                dve.wait_ge(s_ready, i(1))
                nc.vector.tensor_tensor(tile, ps_s[t % 2][:, 0:HK].rearrange("p (h m) -> p h m", h=GH),
                                        sbias[:, b, :, :], ALU.add).then_inc(s_free, 1)
                dve.wait_ge(s_free, i(1 + CREDIT))
                nc.vector.tensor_reduce(row_max[:, t % 2, :], tile, AX.X, ALU.max).then_inc(maxed, 1)
                dve.wait_ge(maxed, i(1))
                nc.vector.tensor_tensor(tile, tile, row_max[:, t % 2, :].unsqueeze(2).to_broadcast([P, GH, KEYS]),
                                        ALU.subtract).then_inc(shifted, 1)

            def normalise(q, g, t):
                i = lambda k: q * (GROUPS * TILES) + g * TILES + (t + k)
                tile = probs[:, t % 4, :].rearrange("p (h m) -> p h m", h=GH)
                dve.wait_ge(exped, i(1))
                nc.vector.tensor_reduce(row_sum[:, t % 2, :], tile, AX.X, ALU.add).then_inc(summed, 1)
                dve.wait_ge(summed, i(1))
                nc.vector.reciprocal(row_sum[:, t % 2, :], row_sum[:, t % 2, :]).then_inc(inverted, 1)
                dve.wait_ge(inverted, i(1))
                nc.vector.tensor_tensor(tile, tile, row_sum[:, t % 2, :].unsqueeze(2).to_broadcast([P, GH, KEYS]),
                                        ALU.mult).then_inc(probs_ready, 1)

            dve.wait_ge(tanh_ready, 1)
            with dve.Fori(0, PASSES) as q:
                layer_norm(q, 0)
                with dve.Fori(0, GROUPS) as g:
                    hi = lambda n: q * W_HI_PASS + g * (W_M + W_V) + (W_LN + n)
                    for n in range(W_C):
                        dve.wait_ge(w_ready, w_at(q, g, n + 1))
                        nc.vector.tensor_copy(sbias[:, :, 2 * n:2 * n + 2, :],
                                              wide[G_BANKS[n]][:, 0:2 * PK].rearrange("p (h b m) -> p b h m", h=2, b=PB))\
                            .then_inc(w_free, 1)
                    for n in range(W_M):
                        h, c4 = divmod(n, 2)
                        cols = (slice(None), slice(4 * c4, 4 * c4 + 4), slice(None), slice(h * KEYS, (h + 1) * KEYS))
                        dve.wait_ge(w_hi, hi(n + 1))
                        nc.vector.tensor_tensor(m_lo[cols], wide[G_BANKS[W_C + n]][:, :]
                                                .rearrange("p (c b k) -> p c b k", c=4, b=PB), m_hi[cols].bitcast(F32), ALU.subtract).then_inc(w_free, 1)
                    for n in range(W_V):
                        k, b, half = n // (2 * PB), n // 2 % PB, n % 2
                        cols = (slice(None), b, k, slice(half * HALF, (half + 1) * HALF))
                        dve.wait_ge(w_hi, hi(W_M + n + 1))
                        nc.vector.tensor_tensor(v_lo[cols], wide[G_BANKS[W_C + W_M + n]][:, :], v_hi[cols].bitcast(F32),
                                                ALU.subtract).then_inc(w_free, 1)
                    dve.wait_ge(bias_added, q * (2 * TILES) + TILES)
                    for k in range(TILES + 3):
                        if k < TILES:
                            biased_scores(q, g, k)
                        if 0 <= k - 1 < TILES:
                            normalise(q, g, k - 1)
                        if 0 <= k - 2 < TILES:
                            t = k - 2
                            dve.wait_ge(pt_hi_ready, q * (GROUPS * TILES) + g * TILES + (t + 1))
                            nc.vector.tensor_tensor(pt_lo[:, t % 2, :, :].rearrange("p c n -> p (c n)"),
                                                    ps_t[t % 2][:, 0:HK],
                                                    pt_hi[:, t % 2, :, :].rearrange("p c n -> p (c n)").bitcast(F32),
                                                    ALU.subtract).then_inc(t_free, 1)
                        if k >= 3:
                            t = k - 3
                            for half in range(2):
                                cols = slice(half * HALF, (half + 1) * HALF)
                                dve.wait_ge(o_ready, q * (2 * GROUPS * TILES) + g * (2 * TILES) + (2 * t + half + 1))
                                nc.vector.scalar_tensor_tensor(out=acc[:, t, cols], in0=ps_o[half][:, :],
                                                               scalar=tanh_g[:, 0:1], in1=acc[:, t, cols],
                                                               op0=ALU.mult, op1=ALU.add).then_inc(o_free, 1)
                dve.wait_ge(o_free, (q + 1) * (2 * GROUPS * TILES) + CREDIT)
                layer_norm(q, 1)

                with dve.Fori(0, FC) as f:
                    for k in range(2):
                        dve.wait_ge(silu_ready, q * (2 * FC) + f * 2 + (k + 1 + CREDIT))
                        dve.wait_ge(lin_ready, q * (2 * FC) + f * 2 + (k + 1))
                        dve.wait_ge(hid_lo, q * (2 * FC) + f * 2 + (k + 1))
                        nc.vector.scalar_tensor_tensor(out=hid_sb[:, k, :], in0=ps_o[k][:, :],
                                                       scalar=b12_sb[:, bass.ds(f + FC, 1)], in1=silu_sb[:, k, :],
                                                       op0=ALU.add, op1=ALU.mult).then_inc(hid_ready, 1)
                    for k in range(2):
                        dve.wait_ge(hid_hi, q * (2 * FC) + f * 2 + (k + 1))
                        tok = slice(k * HALF, (k + 1) * HALF)
                        nc.vector.tensor_tensor(h_lo[:, bass.ds(f, 1), tok].rearrange("p c n -> p (c n)"),
                                                hid_sb[:, k, :],
                                                h_hi[:, bass.ds(f, 1), tok].rearrange("p c n -> p (c n)").bitcast(F32),
                                                ALU.subtract).then_inc(hid_lo, 1)
                for n in range(F2N):
                    dve.wait_ge(t_ready, q * T_PASS + (GROUPS * TILES + n + 1))
                    dve.wait_ge(resid_in[n % 4], q * (16 * F2N // 4) + (16 * (n // 4) + 16))
                    nc.vector.scalar_tensor_tensor(out=resid[:, n % 4, :], in0=ps_t[n % 2][:, :],
                                                   scalar=tanh_g[:, 1:2], in1=resid[:, n % 4, :],
                                                   op0=ALU.mult, op1=ALU.add).then_inc(t_free, 1)


def kernel(**inputs):
    import concourse.bacc as bacc
    from concourse.bass_utils import run_bass_kernel_spmd

    a = {k: np.asarray(v) for k, v in inputs.items()}
    every = lambda v: np.ascontiguousarray(np.broadcast_to(v.reshape(1, -1), (P, v.size)))
    cols = lambda v: np.ascontiguousarray(v.reshape(-1, P).T)

    def units(w):
        k, n = w.shape
        return np.ascontiguousarray(w.reshape(k // P, P, n // P, P).transpose(2, 1, 0, 3)).reshape(n // P, P, k)

    ctx = a["ctx_4096"].reshape(BATCH * KEYS, HID)
    arrays = {
        "x": np.ascontiguousarray(a["x"].reshape(BATCH * SEQ, HID)),
        "ctx_t": np.ascontiguousarray(ctx.T.reshape(MC, P, -1).transpose(1, 0, 2)).reshape(P, -1),
        "g_xattn": every(a["g_xattn"]),
        "g_ffn": every(a["g_ffn"]),
        "wq_t": np.ascontiguousarray(a["L0_xattn_Wq"].T),
        "bq": np.ascontiguousarray(a["L0_xattn_bq"].reshape(GROUPS, GH, P).transpose(0, 2, 1)),
        "wkv": units(a["L0_xattn_Wkv"]),
        "bkv": cols(a["L0_xattn_bkv"]),
        "wo": np.ascontiguousarray(a["L0_xattn_Wo"]),
        "bo": every(a["L0_xattn_bo"]),
        "w12": units(a["L0_ffn_w12"].T),
        "b12": cols(a["L0_ffn_b12"]),
        "w3": np.ascontiguousarray(a["L0_ffn_w3"].T),
        "b3": every(a["L0_ffn_b3"]),
        "ident_in": np.eye(P, dtype=np.float32),
    }
    nc = bacc.Bacc("TRN2", target_bir_lowering=False, num_devices=1)
    aps = {n: nc.dram_tensor(n, v.shape, mybir.dt.from_np(v.dtype), kind="ExternalInput").ap()
           for n, v in arrays.items()}
    out = nc.dram_tensor("out", (BATCH * SEQ, HID), F32, kind="ExternalOutput").ap()
    build(nc, out=out, **aps)
    result = run_bass_kernel_spmd(nc, [arrays], core_ids=[0]).results[0]["out"]
    return result.reshape(BATCH, SEQ, HID)
```

```python
from contextlib import ExitStack

import numpy as np

import concourse.bass as bass
from concourse import mybir

F32 = mybir.dt.float32
F32R = mybir.dt.float32r
ALU = mybir.AluOpType
ACT = mybir.ActivationFunctionType
AX = mybir.AxisListType

P = 128
BATCH, SEQ, HID = 4, 512, 1024
KEYS = 64
HEADS, GROUPS, HDIM = 32, 8, 128
GH = HEADS // GROUPS
PASSES = 2
PB = BATCH // PASSES
PTOK = PB * SEQ
TILES = PTOK // P
BT = SEQ // P
MC = HID // P
FF = 1024
FC = FF // P
HK = GH * KEYS
KC = HK // P
PK = PB * KEYS
HALF = 512
KVJ = 2 * GROUPS
KV_RING = 4
EPS = 1e-5
SCALE = 1.0 / float(np.sqrt(HDIM))

W_KV = KVJ
W_LN = 2 * TILES
W_C, W_M, W_V = 2, GH * 2, PB * KC * 2
W_G = W_C + W_M + W_V
W_PASS = 2 * W_LN + GROUPS * W_G
W_HI_PASS = 2 * W_LN + GROUPS * (W_M + W_V)
G_BANKS = [4, 5] + [0, 1, 2, 3] * (W_M // 4) + [0, 1, 4, 5] * (W_V // 4)
LN2_BANKS = [0, 1, 2, 3] * (W_LN // 8) + [0, 1, 4, 5] * (W_LN // 8)
OPENING = ([("M", n) for n in range(4)] + [("C", n) for n in range(W_C)]
           + [item for t in range(4) for item in (("M", 4 + t), ("T", 2 * t), ("T", 2 * t + 1))])
FIRST = OPENING + [("T", n) for n in range(W_LN // 2, W_LN)] + [("V", n) for n in range(W_V)]
FIRST_BANKS = ([2, 3, 0, 1, 4, 5] + [2, 3, 0, 1] * ((len(OPENING) - 6) // 4)
               + [4, 5, 0, 1] * ((len(FIRST) - len(OPENING)) // 4))
X_SLOTS = (4, 2)
CREDIT = 2
CHAINS = (slice(0, TILES), slice(0, 4), slice(4, 6), slice(6, TILES))
CHAIN_STEPS = 5
LOADS = 5
RES = 3
F2N = 2 * TILES
T_PASS = GROUPS * TILES + F2N
ST_PASS = GROUPS * TILES


def w_at(q, g, n):
    return q * W_PASS + g * W_G + (W_KV + n + W_LN)


def w_first(q, n):
    return q * W_PASS + (W_KV + n)


def w_ln2(q, n):
    return q * W_PASS + (W_KV + n + W_LN + GROUPS * W_G)


def hi_at(q, g, n):
    return q * W_HI_PASS + g * (W_M + W_V) + (n + W_LN)


def hi_first(q, n):
    return q * W_HI_PASS + sum(kind != "C" for kind, _ in FIRST[:n])


def hi_ln2(q, n):
    return q * W_HI_PASS + (n + W_LN + GROUPS * (W_M + W_V))


def freed(banks, n):
    same = [k for k in range(n) if banks[k] == banks[n]]
    return same[-1] + 1 if same else None


def groups(eng, step, stream):
    stream(0, True, False)
    with eng.Fori(1, GROUPS - 1) as g:
        step(g)
        stream(g, False, False)
    step(GROUPS - 1)
    stream(GROUPS - 1, False, True)


def build(nc, x, ctx_t, g_xattn, g_ffn, wq_t, bq, wkv, bkv, wo, bo, w12, b12, w3, b3, ident_in, out):
    with ExitStack() as stack:
        sem = lambda name: stack.enter_context(nc.semaphore(name))
        bank = lambda name: stack.enter_context(nc.psum_tensor(name, [P, HALF], F32))

        KB = 1024
        SIZE = 207 * KB + KB // 2
        stack.enter_context(nc.sbuf_tensor("arena", [P, SIZE // 4], F32))
        base = nc.sbuf_base - SIZE
        top = [0]

        def at(name, shape, dt, offset=None):
            size = 4 * int(np.prod(shape[1:]))
            start = top[0] if offset is None else offset
            if offset is None:
                top[0] += -(-size // 32) * 32
            assert start + size <= SIZE, name
            return nc.alloc_sbuf_tensor_at(name, shape, dt, offset=base + start)

        xt_hi = at("xt_hi", [P, MC, PTOK], F32R)
        xt_lo = at("xt_lo", [P, MC, PTOK], F32R)
        work_at = top[0]
        work_hi = at("work_hi", [P, MC * PTOK], F32R)
        work_lo = at("work_lo", [P, MC * PTOK], F32R)
        attn_at = top[0]
        acc = at("acc", [P, TILES, HID], F32)
        wq_sb = at("wq_sb", [P, GH, HID], F32)
        wo_at = top[0]
        wo_sb = at("wo_sb", [P, GH, HID], F32)
        tmp_at = top[0]
        kvg = at("kvg", [P, 2, PK], F32)
        sbias = at("sbias", [P, PB, GH, KEYS], F32)
        probs = at("probs", [P, 3, HK], F32)
        pt_hi = at("pt_hi", [P, 2, KC, P], F32R)
        pt_lo = at("pt_lo", [P, 2, KC, P], F32R)
        bias_row = at("bias_row", [P, HID], F32)
        ident = at("ident", [P, P], F32)
        bqg = at("bqg", [P, GH], F32)
        bkv_sb = at("bkv_sb", [P, KVJ], F32)
        b12_sb = at("b12_sb", [P, 2 * FC], F32)
        gates = at("gates", [P, 2], F32)
        tanh_g = at("tanh_g", [P, 2], F32)
        stats = at("stats", [P, TILES, 2, 6], F32)
        mean_var = at("mean_var", [P, TILES, 2], F32)
        var_eps = at("var_eps", [P, TILES], F32)
        rstd = at("rstd", [P, TILES], F32)
        square_sum = at("square_sum", [P, TILES], F32)
        shift = at("shift", [P, TILES], F32)
        row_max = at("row_max", [P, 2, GH], F32)
        row_sum = at("row_sum", [P, 2, GH], F32)
        wkv_sb = at("wkv_sb", [P, KVJ, HID], F32, 0)
        wkv_hi = at("wkv_hi", [P, KV_RING, HID], F32R, work_at)
        wkv_lo = at("wkv_lo", [P, KV_RING, HID], F32R, work_at + 16 * KB)
        ctx_hi = at("ctx_hi", [P, MC, BATCH * KEYS], F32R, work_at + 32 * KB)
        ctx_sb = at("ctx_sb", [P, MC, BATCH * KEYS], F32, work_at + 40 * KB)
        ctx_lo = at("ctx_lo", [P, MC, BATCH * KEYS], F32R, work_at + 40 * KB)
        kv_out = at("kv_out", [P, 2, BATCH * KEYS], F32, work_at + 48 * KB)
        w3a_hi = at("w3a_hi", [P, FC, HALF], F32R, attn_at)
        w3a_lo = at("w3a_lo", [P, FC, HALF], F32R, attn_at + 16 * KB)
        w12_hi = at("w12_hi", [P, 2, MC, P], F32R, attn_at + 32 * KB)
        w12_lo = at("w12_lo", [P, 2, MC, P], F32R, attn_at + 40 * KB)
        w12_raw = at("w12_raw", [P, 2, HID], F32, wo_at + 8 * KB)
        silu_sb = at("silu_sb", [P, 2, HALF], F32, tmp_at)
        hid_sb = at("hid_sb", [P, 2, HALF], F32, tmp_at + 4 * KB)
        w3_raw = at("w3_raw", [P, HALF], F32, tmp_at + 8 * KB)
        resid = at("resid", [P, RES, HALF], F32, tmp_at + 3 * KB)

        m_hi = work_hi[:, 0:MC * PB * HK].rearrange("p (c b k) -> p c b k", c=MC, b=PB)
        m_lo = work_lo[:, 0:MC * PB * HK].rearrange("p (c b k) -> p c b k", c=MC, b=PB)
        v_hi = work_hi[:, MC * PB * HK:].rearrange("p (b c n) -> p b c n", b=PB, c=KC)
        v_lo = work_lo[:, MC * PB * HK:].rearrange("p (b c n) -> p b c n", b=PB, c=KC)
        h_hi = work_hi[:, :].rearrange("p (c t) -> p c t", c=FC)
        h_lo = work_lo[:, :].rearrange("p (c t) -> p c t", c=FC)
        w3b_hi = xt_hi[:, 0:FC // 2, :].rearrange("p c (u n) -> p (c u) n", u=2)
        w3b_lo = xt_lo[:, 0:FC // 2, :].rearrange("p c (u n) -> p (c u) n", u=2)
        x_norm = wo_sb

        ps_w = [bank("ps_w0"), bank("ps_w1")]
        ps_s = [bank("ps_s0"), bank("ps_s1")]
        ps_t = [bank("ps_t0"), bank("ps_t1")]
        wide = ps_w + ps_s + ps_t
        ps_o = [bank("ps_o0"), bank("ps_o1")]

        kv_dram = nc.dram_tensor("kv_scratch", (2, GROUPS, PASSES, P, PK), F32, kind="Internal").ap()
        x1_dram = nc.dram_tensor("x1_scratch", (BATCH * SEQ, HID), F32, kind="Internal").ap()

        kv_store = kv_dram.rearrange("k g q p m -> (k g) p q m")
        kv_load = kv_dram.rearrange("k g q p m -> (g q) p k m")
        x_tiles = x.rearrange("(q t p) n -> q t p n", q=PASSES, p=P)
        x1_tiles = x1_dram.rearrange("(q t p) n -> q t p n", q=PASSES, p=P)
        out_tiles = out.rearrange("(q t p) n -> q t p n", q=PASSES, p=P)
        wq_v = wq_t.rearrange("(g h p) n -> g p h n", g=GROUPS, p=P)
        wo_v = wo.rearrange("(g h p) n -> g p h n", g=GROUPS, p=P)
        w3_v = w3.rearrange("(f p) n -> f p n", p=P)

        consts_in = sem("consts_in")
        passed = sem("passed")
        gates_in = sem("gates_in")
        ctx_in = [sem("ctx_in0"), sem("ctx_in1")]
        ctx_hi_ready = sem("ctx_hi_ready")
        ctx_ready = sem("ctx_ready")
        wkv_hi_ready = [sem(f"wkv_hi_ready{s}") for s in range(KV_RING)]
        wkv_ready = [sem(f"wkv_ready{s}") for s in range(KV_RING)]
        wkv_in = [sem(f"wkv_in{s}") for s in range(4)]
        kv_stored = [sem(f"kv_stored{s}") for s in range(2)]
        x_in = [sem(f"x_in{t}") for t in range(TILES)]
        brow_in = sem("brow_in")
        brow_ready = sem("brow_ready")
        bias_added = sem("bias_added")
        x1_stored = sem("x1_stored")
        wq_in = sem("wq_in")
        wo_in = [sem("wo_in0"), sem("wo_in1")]
        kvg_in = sem("kvg_in")
        tanh_ready = sem("tanh_ready")
        averaged = sem("averaged")
        squared = sem("squared")
        stats_ready = sem("stats_ready")
        var_ready = sem("var_ready")
        ln_step = sem("ln_step")
        std_ready = sem("std_ready")
        norm_ready = sem("norm_ready")
        w_ready = sem("w_ready")
        w_hi = sem("w_hi")
        w_free = sem("w_free")
        s_ready = sem("s_ready")
        s_free = sem("s_free")
        maxed = sem("maxed")
        shifted = sem("shifted")
        exped = sem("exped")
        summed = sem("summed")
        inverted = sem("inverted")
        probs_ready = sem("probs_ready")
        t_ready = sem("t_ready")
        pt_hi_ready = sem("pt_hi_ready")
        t_free = sem("t_free")
        o_ready = sem("o_ready")
        o_free = sem("o_free")
        w12_in = [sem("w12_in0"), sem("w12_in1")]
        w12_hi_ready = [sem("w12_hi_ready0"), sem("w12_hi_ready1")]
        w12_ready = [sem("w12_ready0"), sem("w12_ready1")]
        w3_in = sem("w3_in")
        w3_hi_ready = sem("w3_hi_ready")
        w3_ready = sem("w3_ready")
        w3b_in = [sem("w3b_in0"), sem("w3b_in1")]
        w3b_hi_ready = [sem("w3b_hi_ready0"), sem("w3b_hi_ready1")]
        w3b_ready = [sem("w3b_ready0"), sem("w3b_ready1")]
        gate_ready = sem("gate_ready")
        lin_ready = sem("lin_ready")
        silu_ready = sem("silu_ready")
        hid_ready = sem("hid_ready")
        hid_hi = sem("hid_hi")
        hid_lo = sem("hid_lo")
        resid_in = [sem(f"resid_in{s}") for s in range(RES)]
        half_over = sem("half_over")
        pass_over = sem("pass_over")
        out_stored = [sem(f"out_stored{s}") for s in range(RES)]

        def alone(eng):
            eng.sem_inc(passed, 1)

        block = stack.enter_context(nc.Block())

        in_slot = [len(range(s, F2N, RES)) for s in range(RES)]

        @block.sync
        def _(sp):
            half_ctx = MC // 2
            for s in range(KV_RING):
                sp.dma_start(wkv_sb[:, s, :], wkv[s]).then_inc(wkv_in[s], 16)
                if s == 0:
                    for k in range(2):
                        sp.dma_start(ctx_sb[:, k * half_ctx:(k + 1) * half_ctx, :],
                                     ctx_t.rearrange("p (k c n) -> k p c n", k=2, c=half_ctx)[k])\
                            .then_inc(ctx_in[k], 16)
            sp.dma_start(bkv_sb[:, :], bkv).then_inc(consts_in, 16)
            sp.dma_start(ident[:, :], ident_in).then_inc(consts_in, 16)
            sp.dma_start(b12_sb[:, :], b12).then_inc(consts_in, 16)
            with sp.Fori(1, KVJ // KV_RING) as i:
                for s in range(KV_RING):
                    sp.wait_ge(wkv_hi_ready[s], i)
                    alone(sp)
                    sp.dma_start(wkv_sb[:, bass.ds(i * KV_RING + s, 1), :].rearrange("p c n -> p (c n)"),
                                 wkv[i * KV_RING + s]).then_inc(wkv_in[s], 16)
            for s in range(2):
                sp.wait_ge(kv_stored[s], 16 * KVJ // 2)
            with sp.Fori(0, PASSES) as q:
                for k in range(2):
                    sp.wait_ge(w_ready, w_first(q, FIRST.index(("T", 2 * (5 + 2 * k) + 1)) + 1))
                    alone(sp)
                    sp.dma_start(wo_sb[:, 2 * k:2 * k + 2, :], wo_v[0, :, 2 * k:2 * k + 2, :])\
                        .then_inc(wo_in[k], 16)
                with sp.Fori(1, GROUPS) as g:
                    sp.wait_ge(w_ready, w_at(q, g, -W_V))
                    sp.dma_start(wq_sb[:, :, :], wq_v[g]).then_inc(wq_in, 16)
                    sp.wait_ge(w_ready, w_at(q, g, 0))
                    sp.dma_start(kvg[:, :, :], kv_load[g * PASSES + q]).then_inc(kvg_in, 16)
                    sp.dma_start(bqg[:, :], bq[g]).then_inc(kvg_in, 16)
                    for k in range(2):
                        sp.dma_start(wo_sb[:, 2 * k:2 * k + 2, :], wo_v[g, :, 2 * k:2 * k + 2, :])\
                            .then_inc(wo_in[k], 16)
                sp.wait_ge(bias_added, q * (2 * TILES) + TILES)
                alone(sp)
                sp.dma_start(bias_row[:, :], b3).then_inc(brow_in, 16)
                sp.wait_ge(w_ready, w_at(q, GROUPS - 1, W_G))
                alone(sp)
                with sp.Fori(0, FC) as f:
                    for u in range(2):
                        sp.wait_ge(w12_ready[u], q * FC + f + 1)
                        alone(sp)
                        sp.dma_start(w12_raw[:, u, :], w12[f + u * FC]).then_inc(w12_in[u], 16)
                    sp.wait_ge(w3_ready, q * FC + f + 1)
                    sp.wait_ge(o_ready, (q + 1) * (2 * ST_PASS))
                    alone(sp)
                    sp.dma_start(w3_raw[:, :], w3_v[f, :, 0:HALF]).then_inc(w3_in, 16)
                for u in range(2):
                    sp.wait_ge(w12_ready[u], (q + 1) * FC + 1)
                    alone(sp)
                sp.wait_ge(x1_stored, (q + 1) * (16 * TILES))
                sp.wait_ge(hid_lo, (q + 1) * (2 * FC) + CREDIT)
                sp.wait_ge(w3_ready, (q + 1) * FC + 1)
                alone(sp)
                for n in range(F2N):
                    half, t = divmod(n, TILES)
                    s = n % RES
                    if n < FC:
                        if n >= 2:
                            sp.wait_ge(w3b_ready[n % 2], q * (FC // 2) + n // 2)
                            alone(sp)
                        sp.dma_start(w12_raw[:, n % 2, 0:HALF], w3_v[n, :, HALF:]).then_inc(w3b_in[n % 2], 16)
                    if n >= RES:
                        sp.wait_ge(out_stored[s], q * (16 * in_slot[s]) + 16 * (n // RES))
                        alone(sp)
                    sp.dma_start(resid[:, s, :], x1_tiles[q, t, :, half * HALF:(half + 1) * HALF])\
                        .then_inc(resid_in[s], 16)

        @block.gpsimd
        def _(pool):
            pool.sem_inc(half_over, LOADS)
            pool.sem_inc(pass_over, 1)
            for u in range(2):
                pool.sem_inc(w12_ready[u], 1)
            pool.sem_inc(w3_ready, 1)

            def split_wkv_lo(j, s):
                pool.wait_ge(wkv_hi_ready[s], j)
                alone(pool)
                nc.gpsimd.tensor_tensor(wkv_lo[:, s, :],
                                        wkv_sb[:, bass.ds((j - 1) * KV_RING + s, 1), :]
                                        .rearrange("p c n -> p (c n)"),
                                        wkv_hi[:, s, :].bitcast(F32), ALU.subtract).then_inc(wkv_ready[s], 1)

            def store_kv(i, s):
                pool.wait_ge(w_free, i * KV_RING + (s + 1 + CREDIT))
                alone(pool)
                pool.dma_start(kv_store[i * KV_RING + s],
                               kv_out[:, s % 2, :].rearrange("p (q m) -> p q m", q=PASSES))\
                    .then_inc(kv_stored[s % 2], 16)

            for s in range(0, KV_RING, 2):
                nc.gpsimd.wait_ge(wkv_hi_ready[s], 1)
                nc.gpsimd.tensor_tensor(wkv_lo[:, s, :], wkv_sb[:, s, :], wkv_hi[:, s, :].bitcast(F32),
                                        ALU.subtract).then_inc(wkv_ready[s], 1)
            with pool.Fori(0, KVJ // KV_RING - 1) as i:
                for s in range(KV_RING):
                    store_kv(i, s)
                    if s % 2 == 0:
                        split_wkv_lo(i + 2, s)
            for s in range(KV_RING):
                store_kv(KVJ // KV_RING - 1, s)
            pool.wait_ge(tanh_ready, 1)

            def add_bias(q, which):
                pool.wait_ge(brow_in, q * 32 + (16 * which + 16))
                alone(pool)
                nc.gpsimd.tensor_scalar(bias_row[:, :], bias_row[:, :], tanh_g[:, which:which + 1], None,
                                        ALU.mult).then_inc(brow_ready, 1)
                pool.wait_ge(brow_ready, q * 2 + (which + 1))
                for t in range(TILES):
                    pool.wait_ge(norm_ready, q * (2 * TILES) + (which * TILES + t + 1))
                    nc.gpsimd.tensor_tensor(acc[:, t, :], acc[:, t, :], bias_row[:, :], ALU.add)\
                        .then_inc(bias_added, 1)
                    if which == 1:
                        pool.wait_ge(bias_added, q * (2 * TILES) + (TILES + t + 1))
                        alone(pool)
                        pool.dma_start(x1_tiles[q, t], acc[:, t, :]).then_inc(x1_stored, 16)

            def split_w12_lo(q, f, u):
                pool.wait_ge(w12_hi_ready[u], q * FC + (f + 1))
                nc.gpsimd.tensor_tensor(w12_lo[:, u, :, :].rearrange("p c n -> p (c n)"), w12_raw[:, u, :],
                                        w12_hi[:, u, :, :].rearrange("p c n -> p (c n)").bitcast(F32),
                                        ALU.subtract).then_inc(w12_ready[u], 1)

            def split_w3a_lo(q, f):
                pool.wait_ge(w3_hi_ready, q * FC + (f + 1))
                nc.gpsimd.tensor_tensor(w3a_lo[:, f, :], w3_raw[:, :], w3a_hi[:, f, :].bitcast(F32),
                                        ALU.subtract).then_inc(w3_ready, 1)

            with pool.Fori(0, PASSES) as q:
                add_bias(q, 0)
                for u in range(2):
                    split_w12_lo(q, 0, u)
                add_bias(q, 1)
                with pool.Fori(0, FC) as f:
                    split_w3a_lo(q, f)
                for n in range(F2N):
                    half, t = divmod(n, TILES)
                    s = n % RES
                    if n < FC:
                        pool.wait_ge(w3b_hi_ready[n % 2], q * (FC // 2) + (n // 2 + 1))
                        nc.gpsimd.tensor_tensor(w3b_lo[:, n, :], w12_raw[:, n % 2, 0:HALF],
                                                w3b_hi[:, n, :].bitcast(F32), ALU.subtract)\
                            .then_inc(w3b_ready[n % 2], 1)
                    pool.wait_ge(t_free, q * T_PASS + (ST_PASS + n + 1 + CREDIT))
                    alone(pool)
                    if TILES <= n < TILES + LOADS:
                        pool.sem_inc(half_over, 1)
                    pool.dma_start(out_tiles[q, t, :, half * HALF:(half + 1) * HALF], resid[:, s, :])\
                        .then_inc(out_stored[s], 16)
                for s in range(RES):
                    pool.wait_ge(out_stored[s], (q + 1) * (16 * in_slot[s]))
                    alone(pool)
                pool.sem_inc(pass_over, 1)

        @block.tensor
        def _(pe):
            def three_pass(ps, w_hi_ap, w_lo_ap, m_hi_ap, m_lo_ap, first, last):
                pe.matmul(ps, w_hi_ap, m_hi_ap, start=first, stop=False)
                pe.matmul(ps, w_hi_ap, m_lo_ap, start=False, stop=False)
                return pe.matmul(ps, w_lo_ap, m_hi_ap, start=False, stop=last)

            pe.wait_ge(ctx_ready, 1)
            with pe.Fori(0, KVJ // KV_RING) as i:
                for s in range(KV_RING):
                    pe.wait_ge(wkv_ready[s], i + 1)
                    pe.wait_ge(w_free, i * KV_RING + (s + 1))
                    for c in range(MC):
                        if s == 0 and c == MC // 2:
                            pe.wait_ge(ctx_ready, 2)
                        mm = three_pass(ps_w[s % 2][:, 0:BATCH * KEYS],
                                        wkv_hi[:, s, c * P:(c + 1) * P], wkv_lo[:, s, c * P:(c + 1) * P],
                                        ctx_hi[:, c, :], ctx_lo[:, c, :], c == 0, c == MC - 1)
                    mm.then_inc(w_ready, 1)
            pe.wait_ge(consts_in, 48)

            def transposed(ps, which, n):
                t, half = divmod(n, 2)
                for k in range(4):
                    c = 4 * half + k
                    mm = pe.transpose(ps[:, k * P:(k + 1) * P],
                                      x_norm[:, t % X_SLOTS[which], c * P:(c + 1) * P], ident[:, :])
                mm.then_inc(w_ready, 1)

            def transpose_tokens(q, t):
                pe.wait_ge(norm_ready, q * (2 * TILES) + (TILES + t + 1))
                for n in (2 * t, 2 * t + 1):
                    pe.wait_ge(w_free, w_ln2(q, CREDIT + (freed(LN2_BANKS, n) or 0)))
                    transposed(wide[LN2_BANKS[n]], 1, n)

            def score_bias(ps, n):
                for k in range(2):
                    h = 2 * n + k
                    mm = pe.matmul(ps[:, k * PK:(k + 1) * PK], bqg[:, h:h + 1].to_broadcast([P, P]),
                                   kvg[:, 0, :], start=True, stop=True)
                mm.then_inc(w_ready, 1)

            def key_product(ps, n):
                h, c4 = divmod(n, 2)
                for k in range(4):
                    c = 4 * c4 + k
                    mm = pe.matmul(ps[:, k * PK:(k + 1) * PK], wq_sb[:, h, c * P:(c + 1) * P],
                                   kvg[:, 0, :], start=True, stop=True)
                mm.then_inc(w_ready, 1)

            def value_product(ps, n):
                k, b, half = n // (2 * PB), n // 2 % PB, n % 2
                for u in range(2):
                    mm = pe.matmul(ps[u * KEYS:(u + 1) * KEYS, :], kvg[:, 1, b * KEYS:(b + 1) * KEYS],
                                   wo_sb[:, 2 * k + u, half * HALF:(half + 1) * HALF],
                                   start=True, stop=True)
                mm.then_inc(w_ready, 1)

            def first_items(q, start, count):
                for pos in range(start, start + count):
                    kind, n = FIRST[pos]
                    before = freed(FIRST_BANKS, pos)
                    if kind == "T" and n % 2 == 0:
                        pe.wait_ge(norm_ready, q * (2 * TILES) + (n // 2 + 1))
                    if kind == "V" and n % (W_V // 2) == 0:
                        pe.wait_ge(wo_in[n // (W_V // 2)], q * (16 * GROUPS) + 16)
                    if before is not None:
                        pe.wait_ge(w_free, w_first(q, CREDIT + before))
                    elif FIRST_BANKS[pos] in (0, 1):
                        pe.wait_ge(w_free, w_first(q, CREDIT))
                    elif FIRST_BANKS[pos] in (4, 5):
                        pe.wait_ge(t_free, q * T_PASS + CREDIT)
                    ps = wide[FIRST_BANKS[pos]]
                    if kind == "T":
                        transposed(ps, 0, n)
                    else:
                        {"C": score_bias, "M": key_product, "V": value_product}[kind](ps, n)

            def wide_bank(q, g, n):
                before = freed(G_BANKS, n)
                if before is not None:
                    pe.wait_ge(w_free, w_at(q, g, CREDIT + before))
                elif G_BANKS[n] in (0, 1):
                    pe.wait_ge(w_free, w_at(q, g, CREDIT))
                elif G_BANKS[n] in (2, 3):
                    pe.wait_ge(s_free, q * ST_PASS + g * TILES + CREDIT)
                else:
                    pe.wait_ge(t_free, q * T_PASS + g * TILES + CREDIT)
                return wide[G_BANKS[n]]

            def scores(q, g, t):
                b = t // BT
                tok = slice(t * P, (t + 1) * P)
                pe.wait_ge(s_free, q * ST_PASS + g * TILES + (t + 1))
                for c in range(MC):
                    mm = three_pass(ps_s[t % 2][:, 0:HK], xt_hi[:, c, tok], xt_lo[:, c, tok],
                                    m_hi[:, c, b, :], m_lo[:, c, b, :], c == 0, c == MC - 1)
                mm.then_inc(s_ready, 1)

            def transpose_probs(q, g, t):
                pe.wait_ge(probs_ready, q * ST_PASS + g * TILES + (t + 1))
                pe.wait_ge(t_free, q * T_PASS + g * TILES + (t + 1))
                for k in range(KC):
                    mm = pe.transpose(ps_t[t % 2][:, k * P:(k + 1) * P], probs[:, t % 3, k * P:(k + 1) * P],
                                      ident[:, :])
                mm.then_inc(t_ready, 1)

            def attend(q, g, t):
                b = t // BT
                pe.wait_ge(t_free, q * T_PASS + g * TILES + (t + 1 + CREDIT))
                for half in range(2):
                    cols = slice(half * HALF, (half + 1) * HALF)
                    pe.wait_ge(o_free, q * (2 * ST_PASS) + g * (2 * TILES) + (2 * t + half + 1))
                    for k in range(KC):
                        mm = three_pass(ps_o[half][:, :], pt_hi[:, t % 2, k, :], pt_lo[:, t % 2, k, :],
                                        v_hi[:, b, k, cols], v_lo[:, b, k, cols], k == 0, k == KC - 1)
                    mm.then_inc(o_ready, 1)

            def hidden(q, f, k, woven=None):
                tok = slice(k * HALF, (k + 1) * HALF)
                for u in range(2):
                    if k == 0:
                        pe.wait_ge(w12_ready[u], q * FC + (f + 2))
                    if woven and u == 1:
                        pe.wait_ge(o_free, (q + 1) * (2 * ST_PASS) + CREDIT)
                    pe.wait_ge((silu_ready, hid_ready)[u], q * (2 * FC) + f * 2 + (k + 1))
                    for c in range(MC):
                        mm = three_pass((ps_s, ps_o)[u][k][:, :], w12_hi[:, u, c, :], w12_lo[:, u, c, :],
                                        xt_hi[:, c, tok], xt_lo[:, c, tok], c == 0, c == MC - 1)
                        if c == MC - 1:
                            mm.then_inc((gate_ready, lin_ready)[u], 1)
                        if woven and (u, c) in woven:
                            transpose_tokens(q, woven[(u, c)])

            with pe.Fori(0, PASSES) as q:
                def step(g):
                    pe.wait_ge(kvg_in, q * (32 * GROUPS) + (g * 32 + 32))
                    for n in range(W_C):
                        score_bias(wide_bank(q, g, n), n)
                    pe.wait_ge(wq_in, q * (16 * GROUPS) + (g * 16 + 16))
                    for n in range(W_M):
                        key_product(wide_bank(q, g, W_C + n), n)
                    for n in range(W_V):
                        if n % (W_V // 2) == 0:
                            pe.wait_ge(wo_in[n // (W_V // 2)], q * (16 * GROUPS) + (g * 16 + 16))
                        value_product(wide_bank(q, g, W_C + W_M + n), n)

                def stream(g, first, last):
                    if first:
                        pe.wait_ge(kvg_in, q * (32 * GROUPS) + 32)
                        pe.wait_ge(wq_in, q * (16 * GROUPS) + 16)
                        first_items(q, 0, len(OPENING))
                        pe.wait_ge(w_free, w_first(q, FIRST.index(("M", W_M - 1)) + 1 + CREDIT))
                    else:
                        pe.wait_ge(w_free, w_at(q, g, W_C + W_M + CREDIT))
                    for k in range(TILES + 3):
                        if k < TILES:
                            if first:
                                pe.wait_ge(w_free, w_first(q, FIRST.index(("T", 2 * k + 1)) + 1 + CREDIT))
                            scores(q, g, k)
                        if first and k < 2:
                            first_items(q, len(OPENING) + 4 * k, 4)
                        if first and k == 2:
                            first_items(q, len(OPENING) + 8, W_V)
                        if k == 2:
                            pe.wait_ge(w_free, w_first(q, len(FIRST) + CREDIT) if first
                                       else w_at(q, g, W_G + CREDIT))
                        if last and k == TILES + 1:
                            transpose_tokens(q, 0)
                        if 0 <= k - 2 < TILES:
                            transpose_probs(q, g, k - 2)
                        if last and k == TILES + 1:
                            transpose_tokens(q, 1)
                        if last and k == TILES + 2:
                            transpose_tokens(q, 2)
                            transpose_tokens(q, 3)
                        if k >= 3:
                            attend(q, g, k - 3)

                groups(pe, step, stream)
                pe.wait_ge(w_free, w_ln2(q, W_LN // 2 + CREDIT))
                hidden(q, 0, 0, {(0, MC - 1): 4, (1, 1): 5, (1, 3): 6, (1, 5): 7})
                pe.wait_ge(w_free, w_ln2(q, W_LN + CREDIT))
                hidden(q, 0, 1)
                with pe.Fori(1, FC) as f:
                    hidden(q, f, 0)
                    hidden(q, f, 1)
                pe.wait_ge(w3_ready, (q + 1) * FC)
                pe.wait_ge(hid_lo, (q + 1) * (2 * FC) + (CREDIT - 2))
                for n in range(F2N):
                    half, t = divmod(n, TILES)
                    if half == 1 and t == 0:
                        for s in range(2):
                            pe.wait_ge(w3b_ready[s], (q + 1) * (FC // 2))
                    pe.wait_ge(t_free, q * T_PASS + (ST_PASS + n + 1))
                    tok = slice(t * P, (t + 1) * P)
                    w3_hi_half, w3_lo_half = ((w3a_hi, w3a_lo), (w3b_hi, w3b_lo))[half]
                    if n == 1:
                        pe.wait_ge(hid_lo, (q + 1) * (2 * FC) + CREDIT)
                    for f in range(FC):
                        if n == 0 and f == FC - 1:
                            pe.wait_ge(w3_ready, (q + 1) * FC + 1)
                            pe.wait_ge(hid_lo, (q + 1) * (2 * FC) + (CREDIT - 1))
                        mm = three_pass(ps_t[n % 2][:, :], h_hi[:, f, tok], h_lo[:, f, tok],
                                        w3_hi_half[:, f, :], w3_lo_half[:, f, :], f == 0, f == FC - 1)
                    mm.then_inc(t_ready, 1)

        @block.scalar
        def _(act):
            act.sem_inc(silu_ready, CREDIT)
            act.dma_start(gates[:, 0:1], g_xattn).then_inc(gates_in, 16)
            act.dma_start(gates[:, 1:2], g_ffn).then_inc(gates_in, 16)
            for k in range(2):
                part = slice(k * (MC // 2), (k + 1) * (MC // 2))
                act.wait_ge(ctx_in[k], 16)
                nc.scalar.activation(ctx_hi[:, part, :], ctx_sb[:, part, :], ACT.Copy).then_inc(ctx_hi_ready, 1)
            act.wait_ge(gates_in, 32)
            nc.scalar.activation(tanh_g[:, :], gates[:, :], ACT.Tanh).then_inc(tanh_ready, 1)

            def moments(q, t):
                i = lambda n: q * TILES + (t + n)
                dump = x_norm[:, t % 2, :]
                act.wait_ge(x_in[t], q * 16 + 16)
                if t >= 1:
                    act.wait_ge(squared, i(0))
                nc.scalar.activation(dump, acc[:, t, :], ACT.Copy, scale=1.0 / HID,
                                     accum_out=mean_var[:, t, 0:1]).then_inc(averaged, 1)
                act.wait_ge(averaged, i(1))
                nc.scalar.activation(dump, acc[:, t, :], ACT.Square, bias=mean_var[:, t, 0:1], scale=-1.0,
                                     accum_out=square_sum[:, t:t + 1]).then_inc(squared, 1)

            def root(q, i):
                act.wait_ge(var_ready, q * len(CHAINS) + (i + 1))
                nc.scalar.activation(rstd[:, CHAINS[i]], var_eps[:, CHAINS[i]], ACT.Sqrt).then_inc(std_ready, 1)

            def normalise_tokens(q, which, t):
                i = 0 if which == 0 else 1 + (t >= 4) + (t >= 6)
                act.wait_ge(ln_step, q * (len(CHAINS) * CHAIN_STEPS) + (i + 1) * CHAIN_STEPS)
                if t >= X_SLOTS[which]:
                    n = 2 * (t - X_SLOTS[which]) + 1
                    act.wait_ge(w_ready, w_ln2(q, n + 1) if which else w_first(q, FIRST.index(("T", n)) + 1))
                nc.scalar.activation(x_norm[:, t % X_SLOTS[which], :], acc[:, t, :], ACT.Identity,
                                     bias=shift[:, t:t + 1], scale=rstd[:, t:t + 1]).then_inc(norm_ready, 1)

            def tokens_hi(ps, n):
                t, half = divmod(n, 2)
                nc.scalar.activation(xt_hi[:, 4 * half:4 * half + 4, t * P:(t + 1) * P],
                                     ps[:, :].rearrange("p (c n) -> p c n", c=4), ACT.Copy).then_inc(w_hi, 1)

            def key_product_hi(ps, n):
                h, c4 = divmod(n, 2)
                nc.scalar.activation(m_hi[:, 4 * c4:4 * c4 + 4, :, h * KEYS:(h + 1) * KEYS],
                                     ps[:, :].rearrange("p (c b k) -> p c b k", c=4, b=PB), ACT.Copy)\
                    .then_inc(w_hi, 1)

            def value_product_hi(ps, n):
                k, b, half = n // (2 * PB), n // 2 % PB, n % 2
                nc.scalar.activation(v_hi[:, b, k, half * HALF:(half + 1) * HALF], ps[:, :], ACT.Copy)\
                    .then_inc(w_hi, 1)

            def first_items_hi(q, start, count):
                for pos in range(start, start + count):
                    kind, n = FIRST[pos]
                    if kind == "C":
                        continue
                    act.wait_ge(w_ready, w_first(q, pos + 1))
                    {"T": tokens_hi, "M": key_product_hi, "V": value_product_hi}[kind](wide[FIRST_BANKS[pos]], n)

            def split_tokens_hi(q, t):
                for n in (2 * t, 2 * t + 1):
                    act.wait_ge(w_ready, w_ln2(q, n + 1))
                    tokens_hi(wide[LN2_BANKS[n]], n)

            def split_w12_hi(q, f, u):
                act.wait_ge(w12_in[u], q * (16 * FC) + (f * 16 + 16))
                nc.scalar.activation(w12_hi[:, u, :, :].rearrange("p c n -> p (c n)"), w12_raw[:, u, :],
                                     ACT.Copy).then_inc(w12_hi_ready[u], 1)

            def silu(q, f, k):
                act.wait_ge(gate_ready, q * (2 * FC) + (f * 2 + (k + 1)))
                alone(act)
                nc.scalar.activation(silu_sb[:, k, :], ps_s[k][:, :], ACT.Silu,
                                     bias=b12_sb[:, bass.ds(f, 1)]).then_inc(silu_ready, 1)

            def hidden_hi(q, f, k):
                act.wait_ge(hid_ready, q * (2 * FC) + (f * 2 + (k + 1 + CREDIT)))
                nc.scalar.activation(h_hi[:, bass.ds(f, 1), k * HALF:(k + 1) * HALF]
                                     .rearrange("p c n -> p (c n)"), hid_sb[:, k, :], ACT.Copy)\
                    .then_inc(hid_hi, 1)

            def hidden_chunk(q, f, split_next):
                silu(q, f, 0)
                hidden_hi(q, f, 0)
                silu(q, f, 1)
                if split_next:
                    split_w12_hi(q, f + 1, 0)
                    act.wait_ge(lin_ready, q * (2 * FC) + (f * 2 + 2))
                    split_w12_hi(q, f + 1, 1)
                hidden_hi(q, f, 1)
                act.wait_ge(w3_in, q * (16 * FC) + (f * 16 + 16))
                act.wait_ge(x1_stored, (q + 1) * (16 * TILES))
                nc.scalar.activation(w3a_hi[:, bass.ds(f, 1), :].rearrange("p c n -> p (c n)"), w3_raw[:, :],
                                     ACT.Copy).then_inc(w3_hi_ready, 1)

            with act.Fori(0, PASSES) as q:
                def step(g):
                    for n in range(W_M):
                        act.wait_ge(w_ready, w_at(q, g, W_C + n + 1))
                        key_product_hi(wide[G_BANKS[W_C + n]], n)
                    for n in range(W_V):
                        act.wait_ge(w_ready, w_at(q, g, W_C + W_M + n + 1))
                        value_product_hi(wide[G_BANKS[W_C + W_M + n]], n)

                def stream(g, first, last):
                    def exponentials(k):
                        act.wait_ge(shifted, q * ST_PASS + g * TILES + (k + 1))
                        nc.scalar.activation(probs[:, k % 3, :], probs[:, k % 3, :], ACT.Exp, scale=SCALE)\
                            .then_inc(exped, 1)

                    if first:
                        root(q, 0)
                        first_items_hi(q, 0, 4)
                        normalise_tokens(q, 0, 0)
                        for t in range(4):
                            first_items_hi(q, 6 + 3 * t, 1)
                            normalise_tokens(q, 0, t + 1)
                            first_items_hi(q, 7 + 3 * t, 2)
                        normalise_tokens(q, 0, 5)
                        first_items_hi(q, len(OPENING), 2)
                        normalise_tokens(q, 0, 6)
                        first_items_hi(q, len(OPENING) + 2, 2)
                        exponentials(0)
                        normalise_tokens(q, 0, 7)
                        first_items_hi(q, len(OPENING) + 4, 2)
                        exponentials(1)
                        first_items_hi(q, len(OPENING) + 6, 2)
                        exponentials(2)
                        first_items_hi(q, len(OPENING) + 8, W_V)
                    for k in range(TILES + 2):
                        if 0 <= k - 2 < TILES:
                            t = k - 2
                            act.wait_ge(t_ready, q * T_PASS + g * TILES + (t + 1))
                            nc.scalar.activation(pt_hi[:, t % 2, :, :].rearrange("p c n -> p (c n)"),
                                                 ps_t[t % 2][:, 0:HK], ACT.Copy).then_inc(pt_hi_ready, 1)
                        if k < TILES and not (first and k <= 2):
                            exponentials(k)
                        if last and k in (3, 4):
                            split_w12_hi(q, 0, k - 3)
                        if last and k == TILES - 1:
                            root(q, 1)
                        if last and k == TILES:
                            normalise_tokens(q, 1, 0)
                            normalise_tokens(q, 1, 1)
                            split_tokens_hi(q, 0)

                for t in range(TILES):
                    act.wait_ge(half_over, q * LOADS + (t // 2 + 1))
                    alone(act)
                    act.wait_ge(w_ready, 3 * t // 2 + 2)
                    act.dma_start(acc[:, t, :], x_tiles[q, t]).then_inc(x_in[t], 16)
                    if t >= 3:
                        moments(q, t - 3)
                act.wait_ge(half_over, q * LOADS + LOADS)
                alone(act)
                act.wait_ge(w_ready, KVJ - 3)
                act.dma_start(wq_sb[:, :, :], wq_v[0]).then_inc(wq_in, 16)
                act.dma_start(bias_row[:, :], bo).then_inc(brow_in, 16)
                act.dma_start(bqg[:, :], bq[0]).then_inc(kvg_in, 16)
                act.wait_ge(kv_stored[0], 16 * (GROUPS // 2 + 1))
                act.dma_start(kvg[:, :, :], kv_load[q]).then_inc(kvg_in, 16)
                for t in range(TILES - 3, TILES):
                    moments(q, t)
                groups(act, step, stream)
                normalise_tokens(q, 1, 2)
                split_tokens_hi(q, 1)
                normalise_tokens(q, 1, 3)
                split_tokens_hi(q, 2)
                split_tokens_hi(q, 3)
                root(q, 2)
                normalise_tokens(q, 1, 4)
                normalise_tokens(q, 1, 5)
                split_tokens_hi(q, 4)
                root(q, 3)
                normalise_tokens(q, 1, 6)
                split_tokens_hi(q, 5)
                normalise_tokens(q, 1, 7)
                split_tokens_hi(q, 6)
                split_tokens_hi(q, 7)
                with act.Fori(0, FC - 1) as f:
                    hidden_chunk(q, f, True)
                hidden_chunk(q, FC - 1, False)
                act.wait_ge(hid_lo, (q + 1) * (2 * FC) + CREDIT)
                for n in range(FC):
                    act.wait_ge(w3b_in[n % 2], q * (16 * FC // 2) + (16 * (n // 2) + 16))
                    nc.scalar.activation(w3b_hi[:, n, :], w12_raw[:, n % 2, 0:HALF], ACT.Copy)\
                        .then_inc(w3b_hi_ready[n % 2], 1)

        @block.vector
        def _(dve):
            for s in (w_free, s_free, t_free, o_free, hid_ready, hid_lo):
                dve.sem_inc(s, CREDIT)

            def split_wkv(load, raw, s):
                dve.wait_ge(wkv_in[s], load * 16)
                alone(dve)
                nc.vector.tensor_copy(wkv_hi[:, s, :], raw).then_inc(wkv_hi_ready[s], 1)
                if s % 2:
                    dve.wait_ge(wkv_hi_ready[s], load)
                    nc.vector.tensor_tensor(wkv_lo[:, s, :], raw, wkv_hi[:, s, :].bitcast(F32), ALU.subtract)\
                        .then_inc(wkv_ready[s], 1)

            def evacuate_kv(j, s):
                nc.vector.tensor_scalar(kv_out[:, s % 2, :], ps_w[s % 2][:, 0:BATCH * KEYS],
                                        bkv_sb[:, bass.ds(j, 1)], None, ALU.add).then_inc(w_free, 1)

            split_wkv(1, wkv_sb[:, 0, :], 0)
            for k in range(2):
                part = slice(k * (MC // 2), (k + 1) * (MC // 2))
                dve.wait_ge(ctx_hi_ready, k + 1)
                nc.vector.tensor_tensor(ctx_lo[:, part, :], ctx_sb[:, part, :], ctx_hi[:, part, :].bitcast(F32),
                                        ALU.subtract).then_inc(ctx_ready, 1)
            for s in range(1, KV_RING):
                split_wkv(1, wkv_sb[:, s, :], s)
            dve.wait_ge(consts_in, 48)
            for s in range(KV_RING):
                dve.wait_ge(w_ready, s + 1)
                if s >= 2:
                    dve.wait_ge(kv_stored[s % 2], 16)
                evacuate_kv(s, s)
                split_wkv(2, wkv_sb[:, KV_RING + s, :], s)
            with dve.Fori(1, KVJ // KV_RING - 1) as i:
                for s in range(KV_RING):
                    dve.wait_ge(w_ready, i * KV_RING + (s + 1))
                    dve.wait_ge(kv_stored[s % 2], i * (16 * KV_RING // 2) + 16 * (s // 2))
                    evacuate_kv(i * KV_RING + s, s)
                    split_wkv(i + 2, wkv_sb[:, bass.ds((i + 1) * KV_RING + s, 1), :]
                              .rearrange("p c n -> p (c n)"), s)
            for s in range(KV_RING):
                dve.wait_ge(w_ready, KVJ - KV_RING + (s + 1))
                dve.wait_ge(kv_stored[s % 2], 16 * ((KVJ - KV_RING + s) // 2))
                evacuate_kv(KVJ - KV_RING + s, s)

            def token_stats(t):
                for half in range(2):
                    last = nc.vector.bn_stats(stats[:, t, half, :], acc[:, t, half * HALF:(half + 1) * HALF])
                return last

            def variances(q, i):
                tiles = CHAINS[i]
                if i == 0:
                    dve.wait_ge(squared, q * TILES + TILES)
                    nc.vector.tensor_scalar(var_eps[:, tiles], square_sum[:, tiles], 1.0 / HID, EPS,
                                            ALU.mult, ALU.add).then_inc(var_ready, 1)
                    return
                at_stat = q * (2 * (len(CHAINS) - 1)) + (2 * (i - 1))
                dve.wait_ge(stats_ready, at_stat + 1)
                alone(dve)
                for t in range(TILES)[tiles]:
                    last = nc.vector.bn_aggr(mean_var[:, t, :], stats[:, t, :, :].rearrange("p a b -> p (a b)"))
                last.then_inc(stats_ready, 1)
                dve.wait_ge(stats_ready, at_stat + 2)
                nc.vector.tensor_scalar(var_eps[:, tiles], mean_var[:, tiles, 1], EPS, None, ALU.add)\
                    .then_inc(var_ready, 1)

            def inverse_roots(q, i):
                at_step = lambda k: q * (len(CHAINS) * CHAIN_STEPS) + (i * CHAIN_STEPS + k)
                tiles = CHAINS[i]
                r, v, w = rstd[:, tiles], var_eps[:, tiles], shift[:, tiles]
                dve.wait_ge(std_ready, q * len(CHAINS) + (i + 1))
                nc.vector.reciprocal(r, r).then_inc(ln_step, 1)
                dve.wait_ge(ln_step, at_step(1))
                nc.vector.tensor_tensor(w, r, r, ALU.mult).then_inc(ln_step, 1)
                dve.wait_ge(ln_step, at_step(2))
                nc.vector.scalar_tensor_tensor(out=w, in0=w, scalar=-0.5, in1=v,
                                               op0=ALU.mult, op1=ALU.mult).then_inc(ln_step, 1)
                dve.wait_ge(ln_step, at_step(3))
                nc.vector.scalar_tensor_tensor(out=r, in0=w, scalar=1.5, in1=r,
                                               op0=ALU.add, op1=ALU.mult).then_inc(ln_step, 1)
                dve.wait_ge(ln_step, at_step(4))
                nc.vector.scalar_tensor_tensor(out=w, in0=mean_var[:, tiles, 0], scalar=-1.0,
                                               in1=r, op0=ALU.mult, op1=ALU.mult).then_inc(ln_step, 1)

            def tokens_lo(ps, n):
                t, half = divmod(n, 2)
                cols = (slice(None), slice(4 * half, 4 * half + 4), slice(t * P, (t + 1) * P))
                nc.vector.tensor_tensor(xt_lo[cols], ps[:, :].rearrange("p (c n) -> p c n", c=4),
                                        xt_hi[cols].bitcast(F32), ALU.subtract).then_inc(w_free, 1)

            def key_product_lo(ps, n):
                h, c4 = divmod(n, 2)
                cols = (slice(None), slice(4 * c4, 4 * c4 + 4), slice(None), slice(h * KEYS, (h + 1) * KEYS))
                nc.vector.tensor_tensor(m_lo[cols], ps[:, :].rearrange("p (c b k) -> p c b k", c=4, b=PB),
                                        m_hi[cols].bitcast(F32), ALU.subtract).then_inc(w_free, 1)

            def value_product_lo(ps, n):
                k, b, half = n // (2 * PB), n // 2 % PB, n % 2
                cols = (slice(None), b, k, slice(half * HALF, (half + 1) * HALF))
                nc.vector.tensor_tensor(v_lo[cols], ps[:, :], v_hi[cols].bitcast(F32), ALU.subtract)\
                    .then_inc(w_free, 1)

            def take_bias(ps, n):
                nc.vector.tensor_copy(sbias[:, :, 2 * n:2 * n + 2, :],
                                      ps[:, 0:2 * PK].rearrange("p (h b m) -> p b h m", h=2, b=PB))\
                    .then_inc(w_free, 1)

            def first_items_lo(q, start, count):
                for pos in range(start, start + count):
                    kind, n = FIRST[pos]
                    if kind == "C":
                        dve.wait_ge(w_ready, w_first(q, pos + 1))
                    else:
                        dve.wait_ge(w_hi, hi_first(q, pos + 1))
                    {"C": take_bias, "T": tokens_lo, "M": key_product_lo, "V": value_product_lo}[kind](
                        wide[FIRST_BANKS[pos]], n)

            def split_tokens_lo(q, t):
                for n in (2 * t, 2 * t + 1):
                    dve.wait_ge(w_hi, hi_ln2(q, n + 1))
                    tokens_lo(wide[LN2_BANKS[n]], n)

            def biased_scores(q, g, t):
                b = t // BT
                i = lambda k: q * ST_PASS + g * TILES + (t + k)
                tile = probs[:, t % 3, :].rearrange("p (h m) -> p h m", h=GH)
                dve.wait_ge(s_ready, i(1))
                nc.vector.tensor_tensor(tile, ps_s[t % 2][:, 0:HK].rearrange("p (h m) -> p h m", h=GH),
                                        sbias[:, b, :, :], ALU.add).then_inc(s_free, 1)
                dve.wait_ge(s_free, i(1 + CREDIT))
                nc.vector.tensor_reduce(row_max[:, t % 2, :], tile, AX.X, ALU.max).then_inc(maxed, 1)
                dve.wait_ge(maxed, i(1))
                nc.vector.tensor_tensor(tile, tile, row_max[:, t % 2, :].unsqueeze(2).to_broadcast([P, GH, KEYS]),
                                        ALU.subtract).then_inc(shifted, 1)

            def normalise(q, g, t):
                i = lambda k: q * ST_PASS + g * TILES + (t + k)
                tile = probs[:, t % 3, :].rearrange("p (h m) -> p h m", h=GH)
                dve.wait_ge(exped, i(1))
                nc.vector.tensor_reduce(row_sum[:, t % 2, :], tile, AX.X, ALU.add).then_inc(summed, 1)
                dve.wait_ge(summed, i(1))
                nc.vector.reciprocal(row_sum[:, t % 2, :], row_sum[:, t % 2, :]).then_inc(inverted, 1)
                dve.wait_ge(inverted, i(1))
                nc.vector.tensor_tensor(tile, tile, row_sum[:, t % 2, :].unsqueeze(2).to_broadcast([P, GH, KEYS]),
                                        ALU.mult).then_inc(probs_ready, 1)

            dve.wait_ge(tanh_ready, 1)
            with dve.Fori(0, PASSES) as q:
                def step(g):
                    for n in range(W_C):
                        dve.wait_ge(w_ready, w_at(q, g, n + 1))
                        take_bias(wide[G_BANKS[n]], n)
                    for n in range(W_M):
                        dve.wait_ge(w_hi, hi_at(q, g, n + 1))
                        key_product_lo(wide[G_BANKS[W_C + n]], n)
                    for n in range(W_V):
                        dve.wait_ge(w_hi, hi_at(q, g, W_M + n + 1))
                        value_product_lo(wide[G_BANKS[W_C + W_M + n]], n)

                def stream(g, first, last):
                    if first:
                        variances(q, 0)
                        first_items_lo(q, 0, 2)
                        inverse_roots(q, 0)
                        first_items_lo(q, 2, len(OPENING) - 2)
                        dve.wait_ge(pass_over, q + 1)
                    for k in range(TILES + 3):
                        if k < TILES:
                            biased_scores(q, g, k)
                        if 0 <= k - 1 < TILES:
                            normalise(q, g, k - 1)
                        if first and k < 2:
                            first_items_lo(q, len(OPENING) + 4 * k, 4)
                        if first and k == 2:
                            first_items_lo(q, len(OPENING) + 8, W_V)
                        if last and k == TILES:
                            inverse_roots(q, 1)
                        if last and k == TILES + 1:
                            split_tokens_lo(q, 0)
                        if 0 <= k - 2 < TILES:
                            t = k - 2
                            dve.wait_ge(pt_hi_ready, q * ST_PASS + g * TILES + (t + 1))
                            nc.vector.tensor_tensor(pt_lo[:, t % 2, :, :].rearrange("p c n -> p (c n)"),
                                                    ps_t[t % 2][:, 0:HK],
                                                    pt_hi[:, t % 2, :, :].rearrange("p c n -> p (c n)").bitcast(F32),
                                                    ALU.subtract).then_inc(t_free, 1)
                        if last and k == TILES + 1:
                            split_tokens_lo(q, 1)
                        if last and k == TILES + 2:
                            split_tokens_lo(q, 2)
                            split_tokens_lo(q, 3)
                        if k >= 3:
                            t = k - 3
                            if first:
                                dve.wait_ge(bias_added, q * (2 * TILES) + (t + 1))
                            for half in range(2):
                                cols = slice(half * HALF, (half + 1) * HALF)
                                dve.wait_ge(o_ready, q * (2 * ST_PASS) + g * (2 * TILES) + (2 * t + half + 1))
                                nc.vector.scalar_tensor_tensor(out=acc[:, t, cols], in0=ps_o[half][:, :],
                                                               scalar=tanh_g[:, 0:1], in1=acc[:, t, cols],
                                                               op0=ALU.mult, op1=ALU.add).then_inc(o_free, 1)
                            if last:
                                dve.wait_ge(o_free, q * (2 * ST_PASS) + g * (2 * TILES) + (2 * t + 2 + CREDIT))
                                done = token_stats(t)
                                for i in range(1, len(CHAINS)):
                                    if t == CHAINS[i].stop - 1:
                                        done.then_inc(stats_ready, 1)
                                        variances(q, i)

                groups(dve, step, stream)
                inverse_roots(q, 2)
                split_tokens_lo(q, 4)
                inverse_roots(q, 3)
                for t in range(5, TILES):
                    split_tokens_lo(q, t)

                def hidden_chunk(f, split_next):
                    def split_w12_lo(u):
                        dve.wait_ge(w12_hi_ready[u], q * FC + (f + 2))
                        nc.vector.tensor_tensor(w12_lo[:, u, :, :].rearrange("p c n -> p (c n)"), w12_raw[:, u, :],
                                                w12_hi[:, u, :, :].rearrange("p c n -> p (c n)").bitcast(F32),
                                                ALU.subtract).then_inc(w12_ready[u], 1)

                    for k in range(2):
                        tok = slice(k * HALF, (k + 1) * HALF)
                        i = lambda n: q * (2 * FC) + (f * 2 + (k + n))
                        dve.wait_ge(silu_ready, i(1 + CREDIT))
                        dve.wait_ge(lin_ready, i(1))
                        dve.wait_ge(hid_lo, i(1))
                        nc.vector.scalar_tensor_tensor(out=hid_sb[:, k, :], in0=ps_o[k][:, :],
                                                       scalar=b12_sb[:, bass.ds(f + FC, 1)], in1=silu_sb[:, k, :],
                                                       op0=ALU.add, op1=ALU.mult).then_inc(hid_ready, 1)
                        if split_next and k == 1:
                            split_w12_lo(1)
                        dve.wait_ge(hid_hi, i(1))
                        nc.vector.tensor_tensor(h_lo[:, bass.ds(f, 1), tok].rearrange("p c n -> p (c n)"),
                                                hid_sb[:, k, :],
                                                h_hi[:, bass.ds(f, 1), tok].rearrange("p c n -> p (c n)").bitcast(F32),
                                                ALU.subtract).then_inc(hid_lo, 1)
                        if split_next and k == 0:
                            split_w12_lo(0)

                with dve.Fori(0, FC - 1) as f:
                    hidden_chunk(f, True)
                hidden_chunk(FC - 1, False)
                for n in range(F2N):
                    s = n % RES
                    dve.wait_ge(t_ready, q * T_PASS + (ST_PASS + n + 1))
                    dve.wait_ge(resid_in[s], q * (16 * in_slot[s]) + (16 * (n // RES) + 16))
                    nc.vector.scalar_tensor_tensor(out=resid[:, s, :], in0=ps_t[n % 2][:, :],
                                                   scalar=tanh_g[:, 1:2], in1=resid[:, s, :],
                                                   op0=ALU.mult, op1=ALU.add).then_inc(t_free, 1)


def kernel(**inputs):
    import concourse.bacc as bacc
    from concourse.bass_utils import run_bass_kernel_spmd

    a = {k: np.asarray(v) for k, v in inputs.items()}
    every = lambda v: np.ascontiguousarray(np.broadcast_to(v.reshape(1, -1), (P, v.size)))
    cols = lambda v: np.ascontiguousarray(v.reshape(-1, P).T)

    def units(w):
        k, n = w.shape
        return np.ascontiguousarray(w.reshape(k // P, P, n // P, P).transpose(2, 1, 0, 3)).reshape(n // P, P, k)

    ctx = a["ctx_4096"].reshape(BATCH * KEYS, HID)
    arrays = {
        "x": np.ascontiguousarray(a["x"].reshape(BATCH * SEQ, HID)),
        "ctx_t": np.ascontiguousarray(ctx.T.reshape(MC, P, -1).transpose(1, 0, 2)).reshape(P, -1),
        "g_xattn": every(a["g_xattn"]),
        "g_ffn": every(a["g_ffn"]),
        "wq_t": np.ascontiguousarray(a["L0_xattn_Wq"].T),
        "bq": np.ascontiguousarray(a["L0_xattn_bq"].reshape(GROUPS, GH, P).transpose(0, 2, 1)),
        "wkv": units(a["L0_xattn_Wkv"]),
        "bkv": cols(a["L0_xattn_bkv"]),
        "wo": np.ascontiguousarray(a["L0_xattn_Wo"]),
        "bo": every(a["L0_xattn_bo"]),
        "w12": units(a["L0_ffn_w12"].T),
        "b12": cols(a["L0_ffn_b12"]),
        "w3": np.ascontiguousarray(a["L0_ffn_w3"].T),
        "b3": every(a["L0_ffn_b3"]),
        "ident_in": np.eye(P, dtype=np.float32),
    }
    nc = bacc.Bacc("TRN2", target_bir_lowering=False, num_devices=1)
    aps = {n: nc.dram_tensor(n, v.shape, mybir.dt.from_np(v.dtype), kind="ExternalInput").ap()
           for n, v in arrays.items()}
    out = nc.dram_tensor("out", (BATCH * SEQ, HID), F32, kind="ExternalOutput").ap()
    build(nc, out=out, **aps)
    result = run_bass_kernel_spmd(nc, [arrays], core_ids=[0]).results[0]["out"]
    return result.reshape(BATCH, SEQ, HID)
```

```python
from contextlib import ExitStack

import numpy as np

import concourse.bass as bass
from concourse import mybir

F32 = mybir.dt.float32
F32R = mybir.dt.float32r
ALU = mybir.AluOpType
ACT = mybir.ActivationFunctionType
AX = mybir.AxisListType

P = 128
BATCH, SEQ, HID = 4, 512, 1024
KEYS = 64
HEADS, GROUPS, HDIM = 32, 8, 128
GH = HEADS // GROUPS
PASSES = 2
PB = BATCH // PASSES
PTOK = PB * SEQ
TILES = PTOK // P
BT = SEQ // P
MC = HID // P
FF = 1024
FC = FF // P
HK = GH * KEYS
KC = HK // P
PK = PB * KEYS
HALF = 512
KVJ = 2 * GROUPS
KV_RING = 4
EPS = 1e-5
SCALE = 1.0 / float(np.sqrt(HDIM))

W_KV = KVJ
W_LN = 2 * TILES
W_C, W_M, W_V = 1, GH * 2, PB * KC * 2
W_G = W_C + W_M + W_V
W_PASS = 2 * W_LN + GROUPS * W_G
W_HI_PASS = 2 * W_LN + GROUPS * (W_M + W_V)
G_BANKS = [4] + [0, 1, 2, 3] * (W_M // 4) + [0, 1, 4, 5] * (W_V // 4)
LN2_BANKS = [0, 1, 2, 3] * (W_LN // 8) + [0, 1, 4, 5] * (W_LN // 8)
OPENING = ([("M", n) for n in range(4)] + [("C", n) for n in range(W_C)]
           + [item for t in range(4) for item in (("M", 4 + t), ("T", 2 * t), ("T", 2 * t + 1))])
FIRST = OPENING + [("T", n) for n in range(W_LN // 2, W_LN)] + [("V", n) for n in range(W_V)]
FIRST_BANKS = ([2, 3, 0, 1, 4] + [2, 3, 0, 1] * ((len(OPENING) - 5) // 4)
               + [4, 5, 0, 1] * ((len(FIRST) - len(OPENING)) // 4))
X_SLOTS = (4, 2)
CREDIT = 2
W_CREDIT = 4
CHAINS = (slice(0, TILES), slice(0, 4), slice(4, 6), slice(6, TILES))
CHAIN_STEPS = 5
LOADS = 5
RES = 3
F2N = 2 * TILES
T_PASS = GROUPS * TILES + F2N
ST_PASS = GROUPS * TILES


def w_at(q, g, n):
    return q * W_PASS + g * W_G + (W_KV + n + W_LN)


def w_first(q, n):
    return q * W_PASS + (W_KV + n)


def w_ln2(q, n):
    return q * W_PASS + (W_KV + n + W_LN + GROUPS * W_G)


def hi_at(q, g, n):
    return q * W_HI_PASS + g * (W_M + W_V) + (n + W_LN)


def hi_first(q, n):
    return q * W_HI_PASS + sum(kind != "C" for kind, _ in FIRST[:n])


def hi_ln2(q, n):
    return q * W_HI_PASS + (n + W_LN + GROUPS * (W_M + W_V))


def freed(banks, n):
    same = [k for k in range(n) if banks[k] == banks[n]]
    return same[-1] + 1 if same else None


def groups(eng, step, stream):
    stream(0, True, False)
    with eng.Fori(1, GROUPS - 1) as g:
        step(g)
        stream(g, False, False)
    step(GROUPS - 1)
    stream(GROUPS - 1, False, True)


def build(nc, x, ctx_t, g_xattn, g_ffn, wq_t, bq, wkv, bkv, wo, bo, w12, b12, w3, b3, ident_in, out):
    with ExitStack() as stack:
        sem = lambda name: stack.enter_context(nc.semaphore(name))
        bank = lambda name: stack.enter_context(nc.psum_tensor(name, [P, HALF], F32))

        KB = 1024
        SIZE = 207 * KB + KB // 2
        stack.enter_context(nc.sbuf_tensor("arena", [P, SIZE // 4], F32))
        base = nc.sbuf_base - SIZE
        top = [0]

        def at(name, shape, dt, offset=None):
            size = 4 * int(np.prod(shape[1:]))
            start = top[0] if offset is None else offset
            if offset is None:
                top[0] += -(-size // 32) * 32
            assert start + size <= SIZE, name
            return nc.alloc_sbuf_tensor_at(name, shape, dt, offset=base + start)

        xt_hi = at("xt_hi", [P, MC, PTOK], F32R)
        xt_lo = at("xt_lo", [P, MC, PTOK], F32R)
        work_at = top[0]
        work_hi = at("work_hi", [P, MC * PTOK], F32R)
        work_lo = at("work_lo", [P, MC * PTOK], F32R)
        attn_at = top[0]
        acc = at("acc", [P, TILES, HID], F32)
        wq_sb = at("wq_sb", [P, GH, HID], F32)
        wo_at = top[0]
        wo_sb = at("wo_sb", [P, GH, HID], F32)
        tmp_at = top[0]
        kvg = at("kvg", [P, 2, PK], F32)
        bias_keys = at("bias_keys", [P, PK], F32, top[0])
        sbias = at("sbias", [P, GH, PB, KEYS], F32)
        probs = at("probs", [P, 3, HK], F32)
        pt_hi = at("pt_hi", [P, 2, KC, P], F32R)
        pt_lo = at("pt_lo", [P, 2, KC, P], F32R)
        bias_row = at("bias_row", [P, HID], F32)
        ident = at("ident", [P, P], F32)
        bqg = at("bqg", [P, GH], F32)
        bkv_sb = at("bkv_sb", [P, KVJ], F32)
        b12_sb = at("b12_sb", [P, 2 * FC], F32)
        gates = at("gates", [P, 2], F32)
        tanh_g = at("tanh_g", [P, 2], F32)
        stats = at("stats", [P, TILES, 2, 6], F32)
        mean_var = at("mean_var", [P, TILES, 2], F32)
        var_eps = at("var_eps", [P, TILES], F32)
        rstd = at("rstd", [P, TILES], F32)
        square_sum = at("square_sum", [P, TILES], F32)
        shift = at("shift", [P, TILES], F32)
        row_max = at("row_max", [P, 2, GH], F32)
        row_sum = at("row_sum", [P, 2, GH], F32)
        wkv_sb = at("wkv_sb", [P, KVJ, HID], F32, 0)
        wkv_hi = at("wkv_hi", [P, KV_RING, HID], F32R, work_at)
        wkv_lo = at("wkv_lo", [P, KV_RING, HID], F32R, work_at + 16 * KB)
        ctx_hi = at("ctx_hi", [P, MC, BATCH * KEYS], F32R, work_at + 32 * KB)
        ctx_sb = at("ctx_sb", [P, MC, BATCH * KEYS], F32, work_at + 40 * KB)
        ctx_lo = at("ctx_lo", [P, MC, BATCH * KEYS], F32R, work_at + 40 * KB)
        kv_out = at("kv_out", [P, KV_RING, BATCH * KEYS], F32, work_at + 48 * KB)
        w3a_hi = at("w3a_hi", [P, FC, HALF], F32R, attn_at)
        w3a_lo = at("w3a_lo", [P, FC, HALF], F32R, attn_at + 16 * KB)
        w12_hi = at("w12_hi", [P, 2, MC, P], F32R, attn_at + 32 * KB)
        w12_lo = at("w12_lo", [P, 2, MC, P], F32R, attn_at + 40 * KB)
        w12_raw = at("w12_raw", [P, 2, HID], F32, wo_at + 8 * KB)
        silu_sb = at("silu_sb", [P, 2, HALF], F32, tmp_at)
        hid_sb = at("hid_sb", [P, 2, HALF], F32, tmp_at + 4 * KB)
        w3_raw = at("w3_raw", [P, HALF], F32, tmp_at + 8 * KB)
        resid = at("resid", [P, RES, HALF], F32, tmp_at + 3 * KB)

        m_hi = work_hi[:, 0:MC * PB * HK].rearrange("p (c b k) -> p c b k", c=MC, b=PB)
        m_lo = work_lo[:, 0:MC * PB * HK].rearrange("p (c b k) -> p c b k", c=MC, b=PB)
        v_hi = work_hi[:, MC * PB * HK:].rearrange("p (b c n) -> p b c n", b=PB, c=KC)
        v_lo = work_lo[:, MC * PB * HK:].rearrange("p (b c n) -> p b c n", b=PB, c=KC)
        h_hi = work_hi[:, :].rearrange("p (c t) -> p c t", c=FC)
        h_lo = work_lo[:, :].rearrange("p (c t) -> p c t", c=FC)
        w3b_hi = xt_hi[:, 0:FC // 2, :].rearrange("p c (u n) -> p (c u) n", u=2)
        w3b_lo = xt_lo[:, 0:FC // 2, :].rearrange("p c (u n) -> p (c u) n", u=2)
        x_norm = wo_sb

        ps_w = [bank("ps_w0"), bank("ps_w1")]
        ps_s = [bank("ps_s0"), bank("ps_s1")]
        ps_t = [bank("ps_t0"), bank("ps_t1")]
        wide = ps_w + ps_s + ps_t
        ps_o = [bank("ps_o0"), bank("ps_o1")]

        kv_dram = nc.dram_tensor("kv_scratch", (2, GROUPS, PASSES, P, PK), F32, kind="Internal").ap()
        x1_dram = nc.dram_tensor("x1_scratch", (BATCH * SEQ, HID), F32, kind="Internal").ap()

        bias_dram = nc.dram_tensor("bias_scratch", (1, GH * PK), F32, kind="Internal").ap()

        kv_store = kv_dram.rearrange("k g q p m -> (k g) p q m")
        kv_load = kv_dram.rearrange("k g q p m -> (g q) p k m")
        x_tiles = x.rearrange("(q t p) n -> q t p n", q=PASSES, p=P)
        x1_tiles = x1_dram.rearrange("(q t p) n -> q t p n", q=PASSES, p=P)
        out_tiles = out.rearrange("(q t p) n -> q t p n", q=PASSES, p=P)
        wq_v = wq_t.rearrange("(g h p) n -> g p h n", g=GROUPS, p=P)
        wo_v = wo.rearrange("(g h p) n -> g p h n", g=GROUPS, p=P)
        w3_v = w3.rearrange("(f p) n -> f p n", p=P)

        consts_in = sem("consts_in")
        passed = sem("passed")
        gates_in = sem("gates_in")
        ctx_in = [sem("ctx_in0"), sem("ctx_in1")]
        ctx_hi_ready = sem("ctx_hi_ready")
        ctx_ready = sem("ctx_ready")
        wkv_hi_ready = [sem(f"wkv_hi_ready{s}") for s in range(KV_RING)]
        wkv_ready = [sem(f"wkv_ready{s}") for s in range(KV_RING)]
        wkv_in = [sem(f"wkv_in{s}") for s in range(4)]
        kv_stored = [sem(f"kv_stored{s}") for s in range(KV_RING)]
        x_in = [sem(f"x_in{t}") for t in range(TILES)]
        brow_in = sem("brow_in")
        brow_ready = sem("brow_ready")
        bias_added = sem("bias_added")
        x1_stored = sem("x1_stored")
        wq_in = sem("wq_in")
        bias_stored = sem("bias_stored")
        sbias_in = sem("sbias_in")
        wo_in = [sem("wo_in0"), sem("wo_in1")]
        kvg_in = sem("kvg_in")
        tanh_ready = sem("tanh_ready")
        averaged = sem("averaged")
        squared = sem("squared")
        stats_ready = sem("stats_ready")
        var_ready = sem("var_ready")
        ln_step = sem("ln_step")
        std_ready = sem("std_ready")
        norm_ready = [sem("norm_ready0"), sem("norm_ready1")]
        w_ready = sem("w_ready")
        w_hi = sem("w_hi")
        w_free = sem("w_free")
        s_ready = sem("s_ready")
        s_free = sem("s_free")
        maxed = sem("maxed")
        shifted = sem("shifted")
        exped = sem("exped")
        summed = sem("summed")
        inverted = sem("inverted")
        probs_ready = sem("probs_ready")
        t_ready = sem("t_ready")
        pt_hi_ready = sem("pt_hi_ready")
        t_free = sem("t_free")
        o_ready = sem("o_ready")
        o_free = sem("o_free")
        w12_in = [sem("w12_in0"), sem("w12_in1")]
        w12_hi_ready = [sem("w12_hi_ready0"), sem("w12_hi_ready1")]
        w12_ready = [sem("w12_ready0"), sem("w12_ready1")]
        w3_in = sem("w3_in")
        w3_hi_ready = sem("w3_hi_ready")
        w3_ready = sem("w3_ready")
        w3b_in = [sem("w3b_in0"), sem("w3b_in1")]
        w3b_hi_ready = [sem("w3b_hi_ready0"), sem("w3b_hi_ready1")]
        w3b_ready = [sem("w3b_ready0"), sem("w3b_ready1")]
        gate_ready = sem("gate_ready")
        lin_ready = sem("lin_ready")
        silu_ready = sem("silu_ready")
        hid_ready = sem("hid_ready")
        hid_hi = sem("hid_hi")
        hid_lo = sem("hid_lo")
        resid_in = [sem(f"resid_in{s}") for s in range(RES)]
        half_over = sem("half_over")
        pass_over = sem("pass_over")
        out_stored = [sem(f"out_stored{s}") for s in range(RES)]

        def alone(eng):
            eng.sem_inc(passed, 1)

        block = stack.enter_context(nc.Block())

        in_slot = [len(range(s, F2N, RES)) for s in range(RES)]

        @block.sync
        def _(sp):
            half_ctx = MC // 2
            for s in range(KV_RING):
                sp.dma_start(wkv_sb[:, s, :], wkv[s]).then_inc(wkv_in[s], 16)
                if s == 0:
                    for k in range(2):
                        sp.dma_start(ctx_sb[:, k * half_ctx:(k + 1) * half_ctx, :],
                                     ctx_t.rearrange("p (k c n) -> k p c n", k=2, c=half_ctx)[k])\
                            .then_inc(ctx_in[k], 16)
            sp.dma_start(bkv_sb[:, :], bkv).then_inc(consts_in, 16)
            sp.dma_start(ident[:, :], ident_in).then_inc(consts_in, 16)
            sp.dma_start(b12_sb[:, :], b12).then_inc(consts_in, 16)
            with sp.Fori(1, KVJ // KV_RING) as i:
                for s in range(KV_RING):
                    sp.wait_ge(wkv_hi_ready[s], i)
                    alone(sp)
                    sp.dma_start(wkv_sb[:, bass.ds(i * KV_RING + s, 1), :].rearrange("p c n -> p (c n)"),
                                 wkv[i * KV_RING + s]).then_inc(wkv_in[s], 16)
            for s in range(KV_RING):
                sp.wait_ge(kv_stored[s], 16 * KVJ // KV_RING)

            def spread_bias(q, g, computed):
                sp.wait_ge(w_free, computed)
                alone(sp)
                sp.dma_start(bias_dram.rearrange("a (h m) -> (a h) m", h=GH), bias_keys[0:GH, :])\
                    .then_inc(bias_stored, 16)
                sp.wait_ge(bias_stored, q * (16 * GROUPS) + (g * 16 + 16))
                alone(sp)
                sp.dma_start(sbias[:, :, :, :].rearrange("p h b m -> p (h b m)"),
                             bias_dram.to_broadcast([P, GH * PK])).then_inc(sbias_in, 16)

            with sp.Fori(0, PASSES) as q:
                spread_bias(q, 0, w_first(q, FIRST.index(("C", 0)) + 1 + W_CREDIT))
                for k in range(2):
                    sp.wait_ge(w_ready, w_first(q, FIRST.index(("T", 2 * (5 + 2 * k) + 1)) + 1))
                    alone(sp)
                    sp.dma_start(wo_sb[:, 2 * k:2 * k + 2, :], wo_v[0, :, 2 * k:2 * k + 2, :])\
                        .then_inc(wo_in[k], 16)
                with sp.Fori(1, GROUPS) as g:
                    sp.wait_ge(w_ready, w_at(q, g, -W_V))
                    sp.dma_start(wq_sb[:, :, :], wq_v[g]).then_inc(wq_in, 16)
                    sp.wait_ge(w_ready, w_at(q, g, 0))
                    sp.dma_start(kvg[:, :, :], kv_load[g * PASSES + q]).then_inc(kvg_in, 16)
                    sp.dma_start(bqg[:, :], bq[g]).then_inc(kvg_in, 16)
                    for k in range(2):
                        sp.dma_start(wo_sb[:, 2 * k:2 * k + 2, :], wo_v[g, :, 2 * k:2 * k + 2, :])\
                            .then_inc(wo_in[k], 16)
                    spread_bias(q, g, w_at(q, g, 1 + W_CREDIT))
                sp.wait_ge(bias_added, q * (2 * TILES) + TILES)
                alone(sp)
                sp.dma_start(bias_row[:, :], b3).then_inc(brow_in, 16)
                sp.wait_ge(w_ready, w_at(q, GROUPS - 1, W_G))
                alone(sp)
                with sp.Fori(0, FC) as f:
                    for u in range(2):
                        sp.wait_ge(w12_ready[u], q * FC + f + 1)
                        alone(sp)
                        sp.dma_start(w12_raw[:, u, :], w12[f + u * FC]).then_inc(w12_in[u], 16)
                    sp.wait_ge(w3_ready, q * FC + f + 1)
                    sp.wait_ge(o_ready, (q + 1) * (2 * ST_PASS))
                    alone(sp)
                    sp.dma_start(w3_raw[:, :], w3_v[f, :, 0:HALF]).then_inc(w3_in, 16)
                for u in range(2):
                    sp.wait_ge(w12_ready[u], (q + 1) * FC + 1)
                    alone(sp)
                sp.wait_ge(x1_stored, (q + 1) * (16 * TILES))
                sp.wait_ge(hid_lo, (q + 1) * (2 * FC) + CREDIT)
                sp.wait_ge(w3_ready, (q + 1) * FC + 1)
                alone(sp)

                def store(n):
                    half, t = divmod(n, TILES)
                    sp.wait_ge(t_free, q * T_PASS + (ST_PASS + n + 1 + CREDIT))
                    alone(sp)
                    sp.dma_start(out_tiles[q, t, :, half * HALF:(half + 1) * HALF], resid[:, n % RES, :])\
                        .then_inc(out_stored[n % RES], 16)

                for n in range(F2N):
                    half, t = divmod(n, TILES)
                    s = n % RES
                    if n < FC:
                        if n >= 2:
                            sp.wait_ge(w3b_ready[n % 2], q * (FC // 2) + n // 2)
                            alone(sp)
                        sp.dma_start(w12_raw[:, n % 2, 0:HALF], w3_v[n, :, HALF:]).then_inc(w3b_in[n % 2], 16)
                    if n >= RES:
                        store(n - RES)
                        sp.wait_ge(out_stored[s], q * (16 * in_slot[s]) + 16 * (n // RES))
                        alone(sp)
                    sp.dma_start(resid[:, s, :], x1_tiles[q, t, :, half * HALF:(half + 1) * HALF])\
                        .then_inc(resid_in[s], 16)
                for n in range(F2N - RES, F2N):
                    store(n)

        @block.gpsimd
        def _(pool):
            pool.sem_inc(half_over, LOADS)
            pool.sem_inc(pass_over, 1)
            for u in range(2):
                pool.sem_inc(w12_ready[u], 1)
            pool.sem_inc(w3_ready, 1)

            def split_wkv_lo(j, s):
                pool.wait_ge(wkv_hi_ready[s], j)
                alone(pool)
                nc.gpsimd.tensor_tensor(wkv_lo[:, s, :],
                                        wkv_sb[:, bass.ds((j - 1) * KV_RING + s, 1), :]
                                        .rearrange("p c n -> p (c n)"),
                                        wkv_hi[:, s, :].bitcast(F32), ALU.subtract).then_inc(wkv_ready[s], 1)

            def store_kv(i, s):
                pool.wait_ge(w_free, i * KV_RING + (s + 1 + W_CREDIT))
                alone(pool)
                pool.dma_start(kv_store[i * KV_RING + s],
                               kv_out[:, s, :].rearrange("p (q m) -> p q m", q=PASSES))\
                    .then_inc(kv_stored[s], 16)

            for s in range(0, KV_RING, 2):
                pool.wait_ge(wkv_hi_ready[s], 1)
                nc.gpsimd.tensor_tensor(wkv_lo[:, s, :], wkv_sb[:, s, :], wkv_hi[:, s, :].bitcast(F32),
                                        ALU.subtract).then_inc(wkv_ready[s], 1)
            with pool.Fori(0, KVJ // KV_RING - 1) as i:
                for s in range(KV_RING):
                    store_kv(i, s)
                    if s % 2 == 0:
                        split_wkv_lo(i + 2, s)
            for s in range(KV_RING):
                store_kv(KVJ // KV_RING - 1, s)
            pool.wait_ge(tanh_ready, 1)

            def add_bias(q, which):
                pool.wait_ge(brow_in, q * 32 + (16 * which + 16))
                alone(pool)
                nc.gpsimd.tensor_scalar(bias_row[:, :], bias_row[:, :], tanh_g[:, which:which + 1], None,
                                        ALU.mult).then_inc(brow_ready, 1)
                pool.wait_ge(brow_ready, q * 2 + (which + 1))
                for t in range(TILES):
                    pool.wait_ge(norm_ready[t % 2], q * TILES + (which * TILES // 2 + t // 2 + 1))
                    nc.gpsimd.tensor_tensor(acc[:, t, :], acc[:, t, :], bias_row[:, :], ALU.add)\
                        .then_inc(bias_added, 1)
                    if which == 1:
                        pool.wait_ge(bias_added, q * (2 * TILES) + (TILES + t + 1))
                        alone(pool)
                        pool.dma_start(x1_tiles[q, t], acc[:, t, :]).then_inc(x1_stored, 16)

            def split_w12_lo(q, f, u):
                pool.wait_ge(w12_hi_ready[u], q * FC + (f + 1))
                nc.gpsimd.tensor_tensor(w12_lo[:, u, :, :].rearrange("p c n -> p (c n)"), w12_raw[:, u, :],
                                        w12_hi[:, u, :, :].rearrange("p c n -> p (c n)").bitcast(F32),
                                        ALU.subtract).then_inc(w12_ready[u], 1)

            def split_w3a_lo(q, f):
                pool.wait_ge(w3_hi_ready, q * FC + (f + 1))
                nc.gpsimd.tensor_tensor(w3a_lo[:, f, :], w3_raw[:, :], w3a_hi[:, f, :].bitcast(F32),
                                        ALU.subtract).then_inc(w3_ready, 1)

            with pool.Fori(0, PASSES) as q:
                add_bias(q, 0)
                for u in range(2):
                    split_w12_lo(q, 0, u)
                add_bias(q, 1)
                with pool.Fori(0, FC) as f:
                    split_w3a_lo(q, f)
                for n in range(TILES + LOADS):
                    if n < FC:
                        pool.wait_ge(w3b_hi_ready[n % 2], q * (FC // 2) + (n // 2 + 1))
                        nc.gpsimd.tensor_tensor(w3b_lo[:, n, :], w12_raw[:, n % 2, 0:HALF],
                                                w3b_hi[:, n, :].bitcast(F32), ALU.subtract)\
                            .then_inc(w3b_ready[n % 2], 1)
                    if n >= TILES:
                        pool.wait_ge(t_free, q * T_PASS + (ST_PASS + n + 1 + CREDIT))
                        alone(pool)
                        pool.sem_inc(half_over, 1)
                for s in range(RES):
                    pool.wait_ge(out_stored[s], (q + 1) * (16 * in_slot[s]))
                    alone(pool)
                pool.sem_inc(pass_over, 1)

        @block.tensor
        def _(pe):
            def three_pass(ps, w_hi_ap, w_lo_ap, m_hi_ap, m_lo_ap, first, last):
                pe.matmul(ps, w_hi_ap, m_hi_ap, start=first, stop=False)
                pe.matmul(ps, w_hi_ap, m_lo_ap, start=False, stop=False)
                return pe.matmul(ps, w_lo_ap, m_hi_ap, start=False, stop=last)

            pe.wait_ge(ctx_ready, 1)
            with pe.Fori(0, KVJ // KV_RING) as i:
                for s in range(KV_RING):
                    pe.wait_ge(wkv_ready[s], i + 1)
                    pe.wait_ge(w_free, i * KV_RING + (s + 1))
                    for c in range(MC):
                        if s == 0 and c == MC // 2:
                            pe.wait_ge(ctx_ready, 2)
                        mm = three_pass(wide[s][:, 0:BATCH * KEYS],
                                        wkv_hi[:, s, c * P:(c + 1) * P], wkv_lo[:, s, c * P:(c + 1) * P],
                                        ctx_hi[:, c, :], ctx_lo[:, c, :], c == 0, c == MC - 1)
                    mm.then_inc(w_ready, 1)
            pe.wait_ge(consts_in, 48)

            def transposed(ps, which, n):
                t, half = divmod(n, 2)
                for k in range(4):
                    c = 4 * half + k
                    mm = pe.transpose(ps[:, k * P:(k + 1) * P],
                                      x_norm[:, t % X_SLOTS[which], c * P:(c + 1) * P], ident[:, :])
                mm.then_inc(w_ready, 1)

            def transpose_tokens(q, t):
                pe.wait_ge(norm_ready[t % 2], q * TILES + (TILES // 2 + t // 2 + 1))
                for n in (2 * t, 2 * t + 1):
                    pe.wait_ge(w_free, w_ln2(q, W_CREDIT + (freed(LN2_BANKS, n) or 0)))
                    transposed(wide[LN2_BANKS[n]], 1, n)

            def score_bias(ps, n):
                pe.matmul(ps[0:GH, 0:PK], bqg[:, :], kvg[:, 0, :], start=True, stop=True).then_inc(w_ready, 1)

            def key_product(ps, n):
                h, c4 = divmod(n, 2)
                for k in range(4):
                    c = 4 * c4 + k
                    mm = pe.matmul(ps[:, k * PK:(k + 1) * PK], wq_sb[:, h, c * P:(c + 1) * P],
                                   kvg[:, 0, :], start=True, stop=True)
                mm.then_inc(w_ready, 1)

            def value_product(ps, n):
                k, b, half = n // (2 * PB), n // 2 % PB, n % 2
                for u in range(2):
                    mm = pe.matmul(ps[u * KEYS:(u + 1) * KEYS, :], kvg[:, 1, b * KEYS:(b + 1) * KEYS],
                                   wo_sb[:, 2 * k + u, half * HALF:(half + 1) * HALF],
                                   start=True, stop=True)
                mm.then_inc(w_ready, 1)

            def first_items(q, start, count):
                for pos in range(start, start + count):
                    kind, n = FIRST[pos]
                    before = freed(FIRST_BANKS, pos)
                    if kind == "T" and n % 2 == 0:
                        pe.wait_ge(norm_ready[n // 2 % 2], q * TILES + (n // 4 + 1))
                    if kind == "V" and n % (W_V // 2) == 0:
                        pe.wait_ge(wo_in[n // (W_V // 2)], q * (16 * GROUPS) + 16)
                    if before is not None:
                        pe.wait_ge(w_free, w_first(q, W_CREDIT + before))
                    elif FIRST_BANKS[pos] < 4:
                        pe.wait_ge(w_free, w_first(q, W_CREDIT - (pos == 0)))
                    elif FIRST_BANKS[pos] in (4, 5):
                        pe.wait_ge(t_free, q * T_PASS + CREDIT)
                    ps = wide[FIRST_BANKS[pos]]
                    if kind == "T":
                        transposed(ps, 0, n)
                    else:
                        {"C": score_bias, "M": key_product, "V": value_product}[kind](ps, n)

            def wide_bank(q, g, n):
                before = freed(G_BANKS, n)
                if before is not None:
                    pe.wait_ge(w_free, w_at(q, g, W_CREDIT + before))
                elif G_BANKS[n] in (0, 1):
                    pe.wait_ge(w_free, w_at(q, g, W_CREDIT))
                elif G_BANKS[n] in (2, 3):
                    pe.wait_ge(s_free, q * ST_PASS + g * TILES + CREDIT)
                else:
                    pe.wait_ge(t_free, q * T_PASS + g * TILES + CREDIT)
                return wide[G_BANKS[n]]

            def scores(q, g, t):
                b = t // BT
                tok = slice(t * P, (t + 1) * P)
                pe.wait_ge(s_free, q * ST_PASS + g * TILES + (t + 1))
                for c in range(MC):
                    mm = three_pass(ps_s[t % 2][:, 0:HK], xt_hi[:, c, tok], xt_lo[:, c, tok],
                                    m_hi[:, c, b, :], m_lo[:, c, b, :], c == 0, c == MC - 1)
                mm.then_inc(s_ready, 1)

            def transpose_probs(q, g, t):
                pe.wait_ge(probs_ready, q * ST_PASS + g * TILES + (t + 1))
                pe.wait_ge(t_free, q * T_PASS + g * TILES + (t + 1))
                for k in range(KC):
                    mm = pe.transpose(ps_t[t % 2][:, k * P:(k + 1) * P], probs[:, t % 3, k * P:(k + 1) * P],
                                      ident[:, :])
                mm.then_inc(t_ready, 1)

            def attend(q, g, t):
                b = t // BT
                pe.wait_ge(t_free, q * T_PASS + g * TILES + (t + 1 + CREDIT))
                for half in range(2):
                    cols = slice(half * HALF, (half + 1) * HALF)
                    pe.wait_ge(o_free, q * (2 * ST_PASS) + g * (2 * TILES) + (2 * t + half + 1))
                    for k in range(KC):
                        mm = three_pass(ps_o[half][:, :], pt_hi[:, t % 2, k, :], pt_lo[:, t % 2, k, :],
                                        v_hi[:, b, k, cols], v_lo[:, b, k, cols], k == 0, k == KC - 1)
                    mm.then_inc(o_ready, 1)

            def hidden(q, f, k, woven=None):
                tok = slice(k * HALF, (k + 1) * HALF)
                for u in range(2):
                    if k == 0:
                        pe.wait_ge(w12_ready[u], q * FC + (f + 2))
                    if woven and u == 1:
                        pe.wait_ge(o_free, (q + 1) * (2 * ST_PASS) + CREDIT)
                    pe.wait_ge((silu_ready, hid_ready)[u], q * (2 * FC) + f * 2 + (k + 1))
                    for c in range(MC):
                        mm = three_pass((ps_s, ps_o)[u][k][:, :], w12_hi[:, u, c, :], w12_lo[:, u, c, :],
                                        xt_hi[:, c, tok], xt_lo[:, c, tok], c == 0, c == MC - 1)
                        if c == MC - 1:
                            mm.then_inc((gate_ready, lin_ready)[u], 1)
                        if woven and (u, c) in woven:
                            transpose_tokens(q, woven[(u, c)])

            with pe.Fori(0, PASSES) as q:
                def step(g):
                    pe.wait_ge(kvg_in, q * (32 * GROUPS) + (g * 32 + 32))
                    for n in range(W_C):
                        score_bias(wide_bank(q, g, n), n)
                    pe.wait_ge(wq_in, q * (16 * GROUPS) + (g * 16 + 16))
                    for n in range(W_M):
                        key_product(wide_bank(q, g, W_C + n), n)
                    for n in range(W_V):
                        if n % (W_V // 2) == 0:
                            pe.wait_ge(wo_in[n // (W_V // 2)], q * (16 * GROUPS) + (g * 16 + 16))
                        value_product(wide_bank(q, g, W_C + W_M + n), n)

                def stream(g, first, last):
                    if first:
                        pe.wait_ge(kvg_in, q * (32 * GROUPS) + 32)
                        pe.wait_ge(wq_in, q * (16 * GROUPS) + 16)
                        first_items(q, 0, len(OPENING))
                        pe.wait_ge(w_free, w_first(q, FIRST.index(("M", W_M - 1)) + 1 + W_CREDIT))
                    else:
                        pe.wait_ge(w_free, w_at(q, g, W_C + W_M + W_CREDIT))
                    for k in range(TILES + 3):
                        if k < TILES:
                            if first:
                                pe.wait_ge(w_free, w_first(q, FIRST.index(("T", 2 * k + 1)) + 1 + W_CREDIT))
                            scores(q, g, k)
                        if first and k < 2:
                            first_items(q, len(OPENING) + 4 * k, 4)
                        if first and k == 2:
                            first_items(q, len(OPENING) + 8, W_V)
                        if first and k == 2:
                            pe.wait_ge(w_free, w_first(q, len(FIRST) - 2 + W_CREDIT))
                        if (first and k == 3) or (not first and k == 2):
                            pe.wait_ge(w_free, w_first(q, len(FIRST) + W_CREDIT) if first
                                       else w_at(q, g, W_G + W_CREDIT))
                        if 0 <= k - 2 < TILES:
                            transpose_probs(q, g, k - 2)
                        if last and k == TILES + 1:
                            transpose_tokens(q, 1)
                        if last and k == TILES + 2:
                            transpose_tokens(q, 3)
                        if k >= 3:
                            attend(q, g, k - 3)
                        if last and k == TILES:
                            transpose_tokens(q, 0)
                        if last and k == TILES + 1:
                            transpose_tokens(q, 2)

                groups(pe, step, stream)
                pe.wait_ge(w_free, w_ln2(q, W_LN // 2 + W_CREDIT))
                hidden(q, 0, 0, {(0, 3): 4, (0, 7): 5, (1, 1): 6, (1, 3): 7})
                pe.wait_ge(w_free, w_ln2(q, W_LN + W_CREDIT))
                hidden(q, 0, 1)
                with pe.Fori(1, FC) as f:
                    hidden(q, f, 0)
                    hidden(q, f, 1)
                pe.wait_ge(w3_ready, (q + 1) * FC)
                pe.wait_ge(hid_lo, (q + 1) * (2 * FC) + (CREDIT - 2))
                for n in range(F2N):
                    half, t = divmod(n, TILES)
                    if half == 1 and t == 0:
                        for s in range(2):
                            pe.wait_ge(w3b_ready[s], (q + 1) * (FC // 2))
                    pe.wait_ge(t_free, q * T_PASS + (ST_PASS + n + 1))
                    tok = slice(t * P, (t + 1) * P)
                    w3_hi_half, w3_lo_half = ((w3a_hi, w3a_lo), (w3b_hi, w3b_lo))[half]
                    if n == 1:
                        pe.wait_ge(hid_lo, (q + 1) * (2 * FC) + CREDIT)
                    for f in range(FC):
                        if n == 0 and f == FC - 1:
                            pe.wait_ge(w3_ready, (q + 1) * FC + 1)
                            pe.wait_ge(hid_lo, (q + 1) * (2 * FC) + (CREDIT - 1))
                        mm = three_pass(ps_t[n % 2][:, :], h_hi[:, f, tok], h_lo[:, f, tok],
                                        w3_hi_half[:, f, :], w3_lo_half[:, f, :], f == 0, f == FC - 1)
                    mm.then_inc(t_ready, 1)

        @block.scalar
        def _(act):
            act.sem_inc(silu_ready, CREDIT)
            act.dma_start(gates[:, 0:1], g_xattn).then_inc(gates_in, 16)
            act.dma_start(gates[:, 1:2], g_ffn).then_inc(gates_in, 16)
            for k in range(2):
                part = slice(k * (MC // 2), (k + 1) * (MC // 2))
                act.wait_ge(ctx_in[k], 16)
                nc.scalar.activation(ctx_hi[:, part, :], ctx_sb[:, part, :], ACT.Copy).then_inc(ctx_hi_ready, 1)
            act.wait_ge(gates_in, 32)
            nc.scalar.activation(tanh_g[:, :], gates[:, :], ACT.Tanh).then_inc(tanh_ready, 1)

            def moments(q, t):
                i = lambda n: q * TILES + (t + n)
                dump = x_norm[:, t % 2, :]
                act.wait_ge(x_in[t], q * 16 + 16)
                if t >= 1:
                    act.wait_ge(squared, i(0))
                nc.scalar.activation(dump, acc[:, t, :], ACT.Copy, scale=1.0 / HID,
                                     accum_out=mean_var[:, t, 0:1]).then_inc(averaged, 1)
                act.wait_ge(averaged, i(1))
                nc.scalar.activation(dump, acc[:, t, :], ACT.Square, bias=mean_var[:, t, 0:1], scale=-1.0,
                                     accum_out=square_sum[:, t:t + 1]).then_inc(squared, 1)

            def root(q, i):
                act.wait_ge(var_ready, q * len(CHAINS) + (i + 1))
                nc.scalar.activation(rstd[:, CHAINS[i]], var_eps[:, CHAINS[i]], ACT.Sqrt).then_inc(std_ready, 1)

            def normalise_tokens(q, which, t):
                i = 0 if which == 0 else 1 + (t >= 4) + (t >= 6)
                act.wait_ge(ln_step, q * (len(CHAINS) * CHAIN_STEPS) + (i + 1) * CHAIN_STEPS)
                if t >= X_SLOTS[which]:
                    n = 2 * (t - X_SLOTS[which]) + 1
                    act.wait_ge(w_ready, w_ln2(q, n + 1) if which else w_first(q, FIRST.index(("T", n)) + 1))
                nc.scalar.activation(x_norm[:, t % X_SLOTS[which], :], acc[:, t, :], ACT.Identity,
                                     bias=shift[:, t:t + 1], scale=rstd[:, t:t + 1]).then_inc(norm_ready[t % 2], 1)

            def tokens_hi(ps, n):
                t, half = divmod(n, 2)
                nc.scalar.activation(xt_hi[:, 4 * half:4 * half + 4, t * P:(t + 1) * P],
                                     ps[:, :].rearrange("p (c n) -> p c n", c=4), ACT.Copy).then_inc(w_hi, 1)

            def key_product_hi(ps, n):
                h, c4 = divmod(n, 2)
                nc.scalar.activation(m_hi[:, 4 * c4:4 * c4 + 4, :, h * KEYS:(h + 1) * KEYS],
                                     ps[:, :].rearrange("p (c b k) -> p c b k", c=4, b=PB), ACT.Copy)\
                    .then_inc(w_hi, 1)

            def value_product_hi(ps, n):
                k, b, half = n // (2 * PB), n // 2 % PB, n % 2
                nc.scalar.activation(v_hi[:, b, k, half * HALF:(half + 1) * HALF], ps[:, :], ACT.Copy)\
                    .then_inc(w_hi, 1)

            def first_items_hi(q, start, count):
                for pos in range(start, start + count):
                    kind, n = FIRST[pos]
                    if kind == "C":
                        continue
                    act.wait_ge(w_ready, w_first(q, pos + 1))
                    {"T": tokens_hi, "M": key_product_hi, "V": value_product_hi}[kind](wide[FIRST_BANKS[pos]], n)

            def split_tokens_hi(q, t):
                for n in (2 * t, 2 * t + 1):
                    act.wait_ge(w_ready, w_ln2(q, n + 1))
                    tokens_hi(wide[LN2_BANKS[n]], n)

            def split_w12_hi(q, f, u):
                act.wait_ge(w12_in[u], q * (16 * FC) + (f * 16 + 16))
                nc.scalar.activation(w12_hi[:, u, :, :].rearrange("p c n -> p (c n)"), w12_raw[:, u, :],
                                     ACT.Copy).then_inc(w12_hi_ready[u], 1)

            def silu(q, f, k):
                act.wait_ge(gate_ready, q * (2 * FC) + (f * 2 + (k + 1)))
                alone(act)
                nc.scalar.activation(silu_sb[:, k, :], ps_s[k][:, :], ACT.Silu,
                                     bias=b12_sb[:, bass.ds(f, 1)]).then_inc(silu_ready, 1)

            def hidden_hi(q, f, k):
                act.wait_ge(hid_ready, q * (2 * FC) + (f * 2 + (k + 1 + CREDIT)))
                nc.scalar.activation(h_hi[:, bass.ds(f, 1), k * HALF:(k + 1) * HALF]
                                     .rearrange("p c n -> p (c n)"), hid_sb[:, k, :], ACT.Copy)\
                    .then_inc(hid_hi, 1)

            def hidden_chunk(q, f, split_next):
                silu(q, f, 0)
                hidden_hi(q, f, 0)
                silu(q, f, 1)
                if split_next:
                    split_w12_hi(q, f + 1, 0)
                    act.wait_ge(lin_ready, q * (2 * FC) + (f * 2 + 2))
                    split_w12_hi(q, f + 1, 1)
                hidden_hi(q, f, 1)
                act.wait_ge(w3_in, q * (16 * FC) + (f * 16 + 16))
                act.wait_ge(x1_stored, (q + 1) * (16 * TILES))
                nc.scalar.activation(w3a_hi[:, bass.ds(f, 1), :].rearrange("p c n -> p (c n)"), w3_raw[:, :],
                                     ACT.Copy).then_inc(w3_hi_ready, 1)

            with act.Fori(0, PASSES) as q:
                def step(g):
                    for n in range(W_M):
                        act.wait_ge(w_ready, w_at(q, g, W_C + n + 1))
                        key_product_hi(wide[G_BANKS[W_C + n]], n)
                    for n in range(W_V):
                        act.wait_ge(w_ready, w_at(q, g, W_C + W_M + n + 1))
                        value_product_hi(wide[G_BANKS[W_C + W_M + n]], n)

                def stream(g, first, last):
                    def exponentials(k):
                        act.wait_ge(shifted, q * ST_PASS + g * TILES + (k + 1))
                        nc.scalar.activation(probs[:, k % 3, :], probs[:, k % 3, :], ACT.Exp, scale=SCALE)\
                            .then_inc(exped, 1)

                    if first:
                        root(q, 0)
                        first_items_hi(q, 0, 3)
                        normalise_tokens(q, 0, 0)
                        first_items_hi(q, 3, 5)
                        normalise_tokens(q, 0, 2)
                        first_items_hi(q, 8, 9)
                        normalise_tokens(q, 0, 4)
                        normalise_tokens(q, 0, 6)
                        first_items_hi(q, len(OPENING), 4)
                        exponentials(0)
                        first_items_hi(q, len(OPENING) + 4, 2)
                        exponentials(1)
                        first_items_hi(q, len(OPENING) + 6, 2)
                        exponentials(2)
                        first_items_hi(q, len(OPENING) + 8, W_V)
                    for k in range(TILES + 2):
                        if 0 <= k - 2 < TILES:
                            t = k - 2
                            act.wait_ge(t_ready, q * T_PASS + g * TILES + (t + 1))
                            nc.scalar.activation(pt_hi[:, t % 2, :, :].rearrange("p c n -> p (c n)"),
                                                 ps_t[t % 2][:, 0:HK], ACT.Copy).then_inc(pt_hi_ready, 1)
                        if last and k == TILES - 1:
                            root(q, 1)
                        if k < TILES and not (first and k <= 2):
                            exponentials(k)
                        if last and k in (3, 4):
                            split_w12_hi(q, 0, k - 3)
                        if last and k == TILES - 1:
                            normalise_tokens(q, 1, 0)
                        if last and k == TILES:
                            normalise_tokens(q, 1, 1)
                            split_tokens_hi(q, 0)
                            normalise_tokens(q, 1, 2)

                for t in range(TILES):
                    act.wait_ge(half_over, q * LOADS + (t // 2 + 1))
                    alone(act)
                    act.wait_ge(w_ready, 5 * t // 4 + 2)
                    act.dma_start(acc[:, t, :], x_tiles[q, t]).then_inc(x_in[t], 16)
                    if t >= 3:
                        moments(q, t - 3)
                act.wait_ge(half_over, q * LOADS + LOADS)
                alone(act)
                act.wait_ge(w_ready, KVJ - 4)
                act.dma_start(wq_sb[:, :, :], wq_v[0]).then_inc(wq_in, 16)
                act.dma_start(bias_row[:, :], bo).then_inc(brow_in, 16)
                act.dma_start(bqg[:, :], bq[0]).then_inc(kvg_in, 16)
                act.wait_ge(kv_stored[0], 16 * (GROUPS // KV_RING + 1))
                act.dma_start(kvg[:, :, :], kv_load[q]).then_inc(kvg_in, 16)
                for t in range(TILES - 3, TILES):
                    moments(q, t)
                groups(act, step, stream)
                split_tokens_hi(q, 1)
                normalise_tokens(q, 1, 3)
                split_tokens_hi(q, 2)
                root(q, 2)
                split_tokens_hi(q, 3)
                normalise_tokens(q, 1, 4)
                normalise_tokens(q, 1, 5)
                split_tokens_hi(q, 4)
                root(q, 3)
                split_tokens_hi(q, 5)
                normalise_tokens(q, 1, 6)
                normalise_tokens(q, 1, 7)
                split_tokens_hi(q, 6)
                split_tokens_hi(q, 7)
                with act.Fori(0, FC - 1) as f:
                    hidden_chunk(q, f, True)
                hidden_chunk(q, FC - 1, False)
                act.wait_ge(hid_lo, (q + 1) * (2 * FC) + CREDIT)
                for n in range(FC):
                    act.wait_ge(w3b_in[n % 2], q * (16 * FC // 2) + (16 * (n // 2) + 16))
                    nc.scalar.activation(w3b_hi[:, n, :], w12_raw[:, n % 2, 0:HALF], ACT.Copy)\
                        .then_inc(w3b_hi_ready[n % 2], 1)

        @block.vector
        def _(dve):
            dve.sem_inc(w_free, W_CREDIT)
            for s in (s_free, t_free, o_free, hid_ready, hid_lo):
                dve.sem_inc(s, CREDIT)

            def split_wkv(load, raw, s):
                dve.wait_ge(wkv_in[s], load * 16)
                alone(dve)
                nc.vector.tensor_copy(wkv_hi[:, s, :], raw).then_inc(wkv_hi_ready[s], 1)
                if s % 2:
                    dve.wait_ge(wkv_hi_ready[s], load)
                    nc.vector.tensor_tensor(wkv_lo[:, s, :], raw, wkv_hi[:, s, :].bitcast(F32), ALU.subtract)\
                        .then_inc(wkv_ready[s], 1)

            def evacuate_kv(j, s):
                nc.vector.tensor_scalar(kv_out[:, s, :], wide[s][:, 0:BATCH * KEYS],
                                        bkv_sb[:, bass.ds(j, 1)], None, ALU.add).then_inc(w_free, 1)

            split_wkv(1, wkv_sb[:, 0, :], 0)
            for k in range(2):
                part = slice(k * (MC // 2), (k + 1) * (MC // 2))
                dve.wait_ge(ctx_hi_ready, k + 1)
                nc.vector.tensor_tensor(ctx_lo[:, part, :], ctx_sb[:, part, :], ctx_hi[:, part, :].bitcast(F32),
                                        ALU.subtract).then_inc(ctx_ready, 1)
            for s in range(1, KV_RING):
                split_wkv(1, wkv_sb[:, s, :], s)
            dve.wait_ge(consts_in, 48)
            for s in range(KV_RING):
                dve.wait_ge(w_ready, s + 1)
                evacuate_kv(s, s)
                split_wkv(2, wkv_sb[:, KV_RING + s, :], s)
            with dve.Fori(1, KVJ // KV_RING - 1) as i:
                for s in range(KV_RING):
                    dve.wait_ge(w_ready, i * KV_RING + (s + 1))
                    dve.wait_ge(kv_stored[s], i * 16)
                    evacuate_kv(i * KV_RING + s, s)
                    split_wkv(i + 2, wkv_sb[:, bass.ds((i + 1) * KV_RING + s, 1), :]
                              .rearrange("p c n -> p (c n)"), s)
            for s in range(KV_RING):
                dve.wait_ge(w_ready, KVJ - KV_RING + (s + 1))
                dve.wait_ge(kv_stored[s], 16 * (KVJ // KV_RING - 1))
                evacuate_kv(KVJ - KV_RING + s, s)

            def token_stats(t):
                for half in range(2):
                    last = nc.vector.bn_stats(stats[:, t, half, :], acc[:, t, half * HALF:(half + 1) * HALF])
                return last

            def variances(q, i):
                tiles = CHAINS[i]
                if i == 0:
                    dve.wait_ge(squared, q * TILES + TILES)
                    nc.vector.tensor_scalar(var_eps[:, tiles], square_sum[:, tiles], 1.0 / HID, EPS,
                                            ALU.mult, ALU.add).then_inc(var_ready, 1)
                    return
                at_stat = q * (2 * (len(CHAINS) - 1)) + (2 * (i - 1))
                dve.wait_ge(stats_ready, at_stat + 1)
                alone(dve)
                for t in range(TILES)[tiles]:
                    last = nc.vector.bn_aggr(mean_var[:, t, :], stats[:, t, :, :].rearrange("p a b -> p (a b)"))
                last.then_inc(stats_ready, 1)
                dve.wait_ge(stats_ready, at_stat + 2)
                nc.vector.tensor_scalar(var_eps[:, tiles], mean_var[:, tiles, 1], EPS, None, ALU.add)\
                    .then_inc(var_ready, 1)

            def inverse_roots(q, i):
                at_step = lambda k: q * (len(CHAINS) * CHAIN_STEPS) + (i * CHAIN_STEPS + k)
                tiles = CHAINS[i]
                r, v, w = rstd[:, tiles], var_eps[:, tiles], shift[:, tiles]
                dve.wait_ge(std_ready, q * len(CHAINS) + (i + 1))
                nc.vector.reciprocal(r, r).then_inc(ln_step, 1)
                dve.wait_ge(ln_step, at_step(1))
                nc.vector.tensor_tensor(w, r, r, ALU.mult).then_inc(ln_step, 1)
                dve.wait_ge(ln_step, at_step(2))
                nc.vector.scalar_tensor_tensor(out=w, in0=w, scalar=-0.5, in1=v,
                                               op0=ALU.mult, op1=ALU.mult).then_inc(ln_step, 1)
                dve.wait_ge(ln_step, at_step(3))
                nc.vector.scalar_tensor_tensor(out=r, in0=w, scalar=1.5, in1=r,
                                               op0=ALU.add, op1=ALU.mult).then_inc(ln_step, 1)
                dve.wait_ge(ln_step, at_step(4))
                nc.vector.scalar_tensor_tensor(out=w, in0=mean_var[:, tiles, 0], scalar=-1.0,
                                               in1=r, op0=ALU.mult, op1=ALU.mult).then_inc(ln_step, 1)

            def normalise_odd_tokens(q, t):
                dve.wait_ge(ln_step, q * (len(CHAINS) * CHAIN_STEPS) + CHAIN_STEPS)
                if t >= X_SLOTS[0]:
                    dve.wait_ge(w_ready, w_first(q, FIRST.index(("T", 2 * (t - X_SLOTS[0]) + 1)) + 1))
                nc.vector.tensor_scalar(x_norm[:, t % X_SLOTS[0], :], acc[:, t, :], rstd[:, t:t + 1],
                                        shift[:, t:t + 1], ALU.mult, ALU.add).then_inc(norm_ready[1], 1)

            def tokens_lo(ps, n):
                t, half = divmod(n, 2)
                cols = (slice(None), slice(4 * half, 4 * half + 4), slice(t * P, (t + 1) * P))
                nc.vector.tensor_tensor(xt_lo[cols], ps[:, :].rearrange("p (c n) -> p c n", c=4),
                                        xt_hi[cols].bitcast(F32), ALU.subtract).then_inc(w_free, 1)

            def key_product_lo(ps, n):
                h, c4 = divmod(n, 2)
                cols = (slice(None), slice(4 * c4, 4 * c4 + 4), slice(None), slice(h * KEYS, (h + 1) * KEYS))
                nc.vector.tensor_tensor(m_lo[cols], ps[:, :].rearrange("p (c b k) -> p c b k", c=4, b=PB),
                                        m_hi[cols].bitcast(F32), ALU.subtract).then_inc(w_free, 1)

            def value_product_lo(ps, n):
                k, b, half = n // (2 * PB), n // 2 % PB, n % 2
                cols = (slice(None), b, k, slice(half * HALF, (half + 1) * HALF))
                nc.vector.tensor_tensor(v_lo[cols], ps[:, :], v_hi[cols].bitcast(F32), ALU.subtract)\
                    .then_inc(w_free, 1)

            def take_bias(ps, n):
                nc.vector.tensor_copy(bias_keys[0:GH, :], ps[0:GH, 0:PK]).then_inc(w_free, 1)

            def first_items_lo(q, start, count):
                for pos in range(start, start + count):
                    kind, n = FIRST[pos]
                    if kind == "C":
                        dve.wait_ge(w_ready, w_first(q, pos + 1))
                    else:
                        dve.wait_ge(w_hi, hi_first(q, pos + 1))
                    {"C": take_bias, "T": tokens_lo, "M": key_product_lo, "V": value_product_lo}[kind](
                        wide[FIRST_BANKS[pos]], n)

            def split_tokens_lo(q, t):
                for n in (2 * t, 2 * t + 1):
                    dve.wait_ge(w_hi, hi_ln2(q, n + 1))
                    tokens_lo(wide[LN2_BANKS[n]], n)

            def softmax(q, g, t):
                i = lambda k: q * ST_PASS + g * TILES + k
                tile = lambda k: probs[:, k % 3, :].rearrange("p (h m) -> p h m", h=GH)
                spread = lambda row: row.unsqueeze(2).to_broadcast([P, GH, KEYS])
                now, before = t < TILES, t >= 1
                if now:
                    dve.wait_ge(s_ready, i(t + 1))
                    nc.vector.tensor_tensor(tile(t), ps_s[t % 2][:, 0:HK].rearrange("p (h m) -> p h m", h=GH),
                                            sbias[:, :, t // BT, :], ALU.add).then_inc(s_free, 1)
                if before:
                    dve.wait_ge(exped, i(t))
                    nc.vector.tensor_reduce(row_sum[:, (t - 1) % 2, :], tile(t - 1), AX.X, ALU.add)\
                        .then_inc(summed, 1)
                if now:
                    dve.wait_ge(s_free, i(t + 1 + CREDIT))
                    nc.vector.tensor_reduce(row_max[:, t % 2, :], tile(t), AX.X, ALU.max).then_inc(maxed, 1)
                if before:
                    dve.wait_ge(summed, i(t))
                    nc.vector.reciprocal(row_sum[:, (t - 1) % 2, :], row_sum[:, (t - 1) % 2, :])\
                        .then_inc(inverted, 1)
                if now:
                    dve.wait_ge(maxed, i(t + 1))
                    nc.vector.tensor_tensor(tile(t), tile(t), spread(row_max[:, t % 2, :]), ALU.subtract)\
                        .then_inc(shifted, 1)
                if before:
                    dve.wait_ge(inverted, i(t))
                    nc.vector.tensor_tensor(tile(t - 1), tile(t - 1), spread(row_sum[:, (t - 1) % 2, :]), ALU.mult)\
                        .then_inc(probs_ready, 1)

            dve.wait_ge(tanh_ready, 1)
            with dve.Fori(0, PASSES) as q:
                def step(g):
                    for n in range(W_C):
                        dve.wait_ge(w_ready, w_at(q, g, n + 1))
                        take_bias(wide[G_BANKS[n]], n)
                    for n in range(W_M):
                        dve.wait_ge(w_hi, hi_at(q, g, n + 1))
                        key_product_lo(wide[G_BANKS[W_C + n]], n)
                    for n in range(W_V):
                        dve.wait_ge(w_hi, hi_at(q, g, W_M + n + 1))
                        value_product_lo(wide[G_BANKS[W_C + W_M + n]], n)

                def stream(g, first, last):
                    if first:
                        variances(q, 0)
                        first_items_lo(q, 0, 1)
                        inverse_roots(q, 0)
                        first_items_lo(q, 1, 2)
                        normalise_odd_tokens(q, 1)
                        first_items_lo(q, 3, 5)
                        normalise_odd_tokens(q, 3)
                        first_items_lo(q, 8, 9)
                        normalise_odd_tokens(q, 5)
                        dve.wait_ge(pass_over, q + 1)
                    dve.wait_ge(sbias_in, q * (16 * GROUPS) + (g * 16 + 16))
                    for k in range(TILES + 3):
                        if k <= TILES:
                            softmax(q, g, k)
                        if first and k < 2:
                            first_items_lo(q, len(OPENING) + 4 * k, 4)
                            if k == 0:
                                normalise_odd_tokens(q, 7)
                        if first and k == 2:
                            first_items_lo(q, len(OPENING) + 8, W_V)
                        if 0 <= k - 2 < TILES:
                            t = k - 2
                            dve.wait_ge(pt_hi_ready, q * ST_PASS + g * TILES + (t + 1))
                            nc.vector.tensor_tensor(pt_lo[:, t % 2, :, :].rearrange("p c n -> p (c n)"),
                                                    ps_t[t % 2][:, 0:HK],
                                                    pt_hi[:, t % 2, :, :].rearrange("p c n -> p (c n)").bitcast(F32),
                                                    ALU.subtract).then_inc(t_free, 1)
                        if last and k == TILES + 1:
                            split_tokens_lo(q, 1)
                        if last and k == TILES + 2:
                            split_tokens_lo(q, 3)
                            inverse_roots(q, 2)
                            dve.wait_ge(o_free, (q + 1) * (2 * ST_PASS) - 2 + CREDIT)
                            token_stats(TILES - 2)
                        if k >= 3:
                            t = k - 3
                            if first:
                                dve.wait_ge(bias_added, q * (2 * TILES) + (t + 1))
                            for half in range(2):
                                cols = slice(half * HALF, (half + 1) * HALF)
                                dve.wait_ge(o_ready, q * (2 * ST_PASS) + g * (2 * TILES) + (2 * t + half + 1))
                                nc.vector.scalar_tensor_tensor(out=acc[:, t, cols], in0=ps_o[half][:, :],
                                                               scalar=tanh_g[:, 0:1], in1=acc[:, t, cols],
                                                               op0=ALU.mult, op1=ALU.add).then_inc(o_free, 1)
                            if last and k == TILES - 1:
                                inverse_roots(q, 1)
                            if last and k == TILES:
                                split_tokens_lo(q, 0)
                            if last and k == TILES + 1:
                                split_tokens_lo(q, 2)
                            if last and t != TILES - 2:
                                dve.wait_ge(o_free, q * (2 * ST_PASS) + g * (2 * TILES) + (2 * t + 2 + CREDIT))
                                done = token_stats(t)
                                for i in range(1, len(CHAINS)):
                                    if t == CHAINS[i].stop - 1:
                                        done.then_inc(stats_ready, 1)
                                        variances(q, i)

                groups(dve, step, stream)
                split_tokens_lo(q, 4)
                inverse_roots(q, 3)
                for t in range(5, TILES):
                    split_tokens_lo(q, t)

                def hidden_chunk(f, split_next):
                    def split_w12_lo(u):
                        dve.wait_ge(w12_hi_ready[u], q * FC + (f + 2))
                        nc.vector.tensor_tensor(w12_lo[:, u, :, :].rearrange("p c n -> p (c n)"), w12_raw[:, u, :],
                                                w12_hi[:, u, :, :].rearrange("p c n -> p (c n)").bitcast(F32),
                                                ALU.subtract).then_inc(w12_ready[u], 1)

                    for k in range(2):
                        tok = slice(k * HALF, (k + 1) * HALF)
                        i = lambda n: q * (2 * FC) + (f * 2 + (k + n))
                        dve.wait_ge(silu_ready, i(1 + CREDIT))
                        dve.wait_ge(lin_ready, i(1))
                        dve.wait_ge(hid_lo, i(1))
                        nc.vector.scalar_tensor_tensor(out=hid_sb[:, k, :], in0=ps_o[k][:, :],
                                                       scalar=b12_sb[:, bass.ds(f + FC, 1)], in1=silu_sb[:, k, :],
                                                       op0=ALU.add, op1=ALU.mult).then_inc(hid_ready, 1)
                        if split_next and k == 1:
                            split_w12_lo(1)
                        dve.wait_ge(hid_hi, i(1))
                        nc.vector.tensor_tensor(h_lo[:, bass.ds(f, 1), tok].rearrange("p c n -> p (c n)"),
                                                hid_sb[:, k, :],
                                                h_hi[:, bass.ds(f, 1), tok].rearrange("p c n -> p (c n)").bitcast(F32),
                                                ALU.subtract).then_inc(hid_lo, 1)
                        if split_next and k == 0:
                            split_w12_lo(0)

                with dve.Fori(0, FC - 1) as f:
                    hidden_chunk(f, True)
                hidden_chunk(FC - 1, False)
                for n in range(F2N):
                    s = n % RES
                    dve.wait_ge(t_ready, q * T_PASS + (ST_PASS + n + 1))
                    dve.wait_ge(resid_in[s], q * (16 * in_slot[s]) + (16 * (n // RES) + 16))
                    nc.vector.scalar_tensor_tensor(out=resid[:, s, :], in0=ps_t[n % 2][:, :],
                                                   scalar=tanh_g[:, 1:2], in1=resid[:, s, :],
                                                   op0=ALU.mult, op1=ALU.add).then_inc(t_free, 1)


def kernel(**inputs):
    import concourse.bacc as bacc
    from concourse.bass_utils import run_bass_kernel_spmd

    a = {k: np.asarray(v) for k, v in inputs.items()}
    every = lambda v: np.ascontiguousarray(np.broadcast_to(v.reshape(1, -1), (P, v.size)))
    cols = lambda v: np.ascontiguousarray(v.reshape(-1, P).T)

    def units(w):
        k, n = w.shape
        return np.ascontiguousarray(w.reshape(k // P, P, n // P, P).transpose(2, 1, 0, 3)).reshape(n // P, P, k)

    ctx = a["ctx_4096"].reshape(BATCH * KEYS, HID)
    arrays = {
        "x": np.ascontiguousarray(a["x"].reshape(BATCH * SEQ, HID)),
        "ctx_t": np.ascontiguousarray(ctx.T.reshape(MC, P, -1).transpose(1, 0, 2)).reshape(P, -1),
        "g_xattn": every(a["g_xattn"]),
        "g_ffn": every(a["g_ffn"]),
        "wq_t": np.ascontiguousarray(a["L0_xattn_Wq"].T),
        "bq": np.ascontiguousarray(a["L0_xattn_bq"].reshape(GROUPS, GH, P).transpose(0, 2, 1)),
        "wkv": units(a["L0_xattn_Wkv"]),
        "bkv": cols(a["L0_xattn_bkv"]),
        "wo": np.ascontiguousarray(a["L0_xattn_Wo"]),
        "bo": every(a["L0_xattn_bo"]),
        "w12": units(a["L0_ffn_w12"].T),
        "b12": cols(a["L0_ffn_b12"]),
        "w3": np.ascontiguousarray(a["L0_ffn_w3"].T),
        "b3": every(a["L0_ffn_b3"]),
        "ident_in": np.eye(P, dtype=np.float32),
    }
    nc = bacc.Bacc("TRN2", target_bir_lowering=False, num_devices=1)
    aps = {n: nc.dram_tensor(n, v.shape, mybir.dt.from_np(v.dtype), kind="ExternalInput").ap()
           for n, v in arrays.items()}
    out = nc.dram_tensor("out", (BATCH * SEQ, HID), F32, kind="ExternalOutput").ap()
    build(nc, out=out, **aps)
    result = run_bass_kernel_spmd(nc, [arrays], core_ids=[0]).results[0]["out"]
    return result.reshape(BATCH, SEQ, HID)
```
